# Optimizing a Trainium2 kernel written in Bass

```python
import numpy as np
import jax
import jax.numpy as jnp

def _softmax(x, axis=-1):
    return jax.nn.softmax(x, axis=axis)

def _gelu(x):
    return jax.nn.gelu(x, approximate=True)

def _silu(x):
    return jax.nn.silu(x)

def _sigmoid(x):
    return jax.nn.sigmoid(x)

def _layernorm(x, axis=-1, eps=1e-05):
    m = jnp.mean(x, axis=axis, keepdims=True)
    v = jnp.var(x, axis=axis, keepdims=True)
    return (x - m) / jnp.sqrt(v + eps)

def _scatter_add(tgt, idx, src, axis=0):
    return tgt.at[idx].add(src)

def _segment_sum(src, seg, n):
    return jax.ops.segment_sum(src, seg, n)
kernel_name = 'mk_cond_resid_d4_seqx_r4_20ee24'

def setup_inputs(seed: int=0):
    np.random.seed(seed)
    _w = jnp.asarray

    def _rec_inputs():
        import jax
        import jax.numpy as jnp
        _rk = jax.random.key(seed)
        x = -0.0003929 + 0.9999 * jax.random.normal(jax.random.fold_in(_rk, 1), (4, 512, 512), jnp.float32)
        _lenS = 512 - jax.random.randint(jax.random.fold_in(_rk, 7), (4,), 0, max(1, 512 // 4) + 1, jnp.int32)
        _lenS2 = 512 - jax.random.randint(jax.random.fold_in(_rk, 8), (4,), 0, max(1, 512 // 4) + 1, jnp.int32)
        cond_2048 = 0.00782532 + 1.00527 * jax.random.normal(jax.random.fold_in(_rk, 11), (4, 512), jnp.float32)
        return (x, cond_2048)
    x, cond_2048 = _rec_inputs()

    def _L0_cond_setup():
        import jax, jax.numpy as jnp
        import numpy as np
        HEADS = 16
        EPS = 1e-06

        def _rms_norm(x, g):
            xf = x.astype(jnp.float32)
            y = xf * jax.lax.rsqrt(jnp.mean(xf * xf, axis=-1, keepdims=True) + EPS)
            return y.astype(x.dtype) * g
        key = jax.random.key(seed)
        ks = jax.random.split(key, 6)
        b, n, dim, emb_dim = (4, 512, 512, 512)
        d_head = dim // HEADS
        return {'x': jax.random.normal(ks[0], (b, n, dim), jnp.float32), 'emb': jax.random.normal(ks[1], (b, 1, emb_dim), jnp.float32), 'W_emb': jax.random.normal(ks[2], (emb_dim, 2 * dim), jnp.float32) * emb_dim ** (-0.5), 'b_emb': jnp.zeros((2 * dim,), jnp.float32), 'g_norm': jnp.ones((dim,), jnp.float32), 'W_qkv': jax.random.normal(ks[3], (dim, 3 * dim), jnp.float32) * dim ** (-0.5), 'g_q': jnp.ones((d_head,), jnp.float32), 'g_k': jnp.ones((d_head,), jnp.float32), 'W_out': jax.random.normal(ks[4], (dim, dim), jnp.float32) * dim ** (-0.5)}
    _L0_cond_all = _L0_cond_setup()
    _L0_cond_in = {k: v for k, v in _L0_cond_all.items() if k in ('W_emb', 'b_emb', 'g_norm', 'W_qkv', 'g_q', 'g_k', 'W_out')}
    del _L0_cond_all

    def _L1_cond_setup():
        import jax, jax.numpy as jnp
        import numpy as np
        B, T, D = (16, 128, 512)
        key = jax.random.key(seed)
        k0, k1, k2, k3 = jax.random.split(key, 4)
        scale = 1.0 / np.sqrt(D)
        return {'initial_state': jax.random.normal(k0, (B, D), jnp.float32), 'inputs': jax.random.normal(k1, (B, T, D), jnp.float32), 'W_ih': jax.random.normal(k2, (D, 3 * D), jnp.float32) * scale, 'W_hh': jax.random.normal(k3, (D, 3 * D), jnp.float32) * scale, 'b_ih': jnp.zeros((3 * D,), jnp.float32), 'b_hh': jnp.zeros((3 * D,), jnp.float32)}
    _L1_cond_all = _L1_cond_setup()
    _L1_cond_in = {k: v for k, v in _L1_cond_all.items() if k in ('W_ih', 'W_hh', 'b_ih', 'b_hh')}
    del _L1_cond_all

    def _L2_cond_setup():
        import jax, jax.numpy as jnp
        import numpy as np
        key = jax.random.key(seed)
        k1, k2 = jax.random.split(key)
        B, T, C, K = (4, 1024, 512, 4)
        x = jax.random.normal(k1, (B, T, C), dtype=jnp.float32)
        w = jax.random.normal(k2, (K, 1, C), dtype=jnp.float32) * 0.1
        return {'x': x, 'w': w}
    _L2_cond_all = _L2_cond_setup()
    _L2_cond_in = {k: v for k, v in _L2_cond_all.items() if k in ()}
    del _L2_cond_all

    def _L3_cond_setup():
        import jax, jax.numpy as jnp
        import numpy as np
        key = jax.random.key(seed)
        k1, k2, k3 = jax.random.split(key, 3)
        B, L, D, K = (4, 1024, 512, 4)
        x = jax.random.normal(k1, (B, L, D), dtype=jnp.float32)
        w = jax.random.normal(k2, (K, 1, D), dtype=jnp.float32) * 0.1
        b = jax.random.normal(k3, (D,), dtype=jnp.float32) * 0.1
        return {'x': x, 'w': w, 'b': b}
    _L3_cond_all = _L3_cond_setup()
    _L3_cond_in = {k: v for k, v in _L3_cond_all.items() if k in ('b',)}
    del _L3_cond_all
    return {'x': x, 'cond_2048': cond_2048, 'L0_cond_W_emb': _L0_cond_in['W_emb'], 'L0_cond_b_emb': _L0_cond_in['b_emb'], 'L0_cond_g_norm': _L0_cond_in['g_norm'], 'L0_cond_W_qkv': _L0_cond_in['W_qkv'], 'L0_cond_g_q': _L0_cond_in['g_q'], 'L0_cond_g_k': _L0_cond_in['g_k'], 'L0_cond_W_out': _L0_cond_in['W_out'], 'L1_cond_W_ih': _L1_cond_in['W_ih'], 'L1_cond_W_hh': _L1_cond_in['W_hh'], 'L1_cond_b_ih': _L1_cond_in['b_ih'], 'L1_cond_b_hh': _L1_cond_in['b_hh'], 'L3_cond_b': _L3_cond_in['b']}

def reference(x, cond_2048, L0_cond_W_emb, L0_cond_b_emb, L0_cond_g_norm, L0_cond_W_qkv, L0_cond_g_q, L0_cond_g_k, L0_cond_W_out, L1_cond_W_ih, L1_cond_W_hh, L1_cond_b_ih, L1_cond_b_hh, L3_cond_b):
    import jax
    import jax.numpy as jnp

    def _L0_cond_ref(x, emb, W_emb, b_emb, g_norm, W_qkv, g_q, g_k, W_out):
        import jax, jax.numpy as jnp
        import numpy as np
        HEADS = 16
        EPS = 1e-06

        def _rms_norm(x, g):
            xf = x.astype(jnp.float32)
            y = xf * jax.lax.rsqrt(jnp.mean(xf * xf, axis=-1, keepdims=True) + EPS)
            return y.astype(x.dtype) * g
        b, n, dim = x.shape
        h = HEADS
        d = dim // h
        scale_shift = emb @ W_emb + b_emb
        scale, shift = jnp.split(scale_shift, 2, axis=-1)
        xn = _rms_norm(x, g_norm) * (1.0 + scale) + shift
        qkv = xn @ W_qkv
        qkv = qkv.reshape(b, n, 3, h, d)
        q, k, v = jnp.moveaxis(qkv, 2, 0)
        q = jnp.swapaxes(q, 1, 2)
        k = jnp.swapaxes(k, 1, 2)
        v = jnp.swapaxes(v, 1, 2)
        q = _rms_norm(q, g_q)
        k = _rms_norm(k, g_k)
        logits = jnp.einsum('bhqd,bhkd->bhqk', q, k) * d ** (-0.5)
        attn = jax.nn.softmax(logits, axis=-1)
        o = jnp.einsum('bhqk,bhkd->bhqd', attn, v)
        o = jnp.swapaxes(o, 1, 2).reshape(b, n, dim)
        return o + o @ W_out

    def _L1_cond_ref(initial_state, inputs, W_ih, W_hh, b_ih, b_hh):
        import jax, jax.numpy as jnp
        import numpy as np
        B, T, D = (16, 128, 512)
        "ScanOverTime(GRU cell): sequential per-timestep module call with\n            dict-state passing; merge_dict_trees stacks the per-step\n            'state_predicted' tensors along axis=1 -> [B, T, D]."

        def cell(h, x):
            gi = x @ W_ih + b_ih
            gh = h @ W_hh + b_hh
            i_r, i_z, i_n = jnp.split(gi, 3, axis=-1)
            h_r, h_z, h_n = jnp.split(gh, 3, axis=-1)
            r = jax.nn.sigmoid(i_r + h_r)
            z = jax.nn.sigmoid(i_z + h_z)
            n = jnp.tanh(i_n + r * h_n)
            h_new = (1.0 - z) * n + z * h
            return (h_new, h_new)
        xs = jnp.swapaxes(inputs, 0, 1)
        _, hs = jax.lax.scan(cell, initial_state, xs)
        return jnp.swapaxes(hs, 0, 1)

    def _L2_cond_ref(x, w):
        import jax, jax.numpy as jnp
        import numpy as np
        K = w.shape[0]
        C = x.shape[-1]
        y = jax.lax.conv_general_dilated(x, w, window_strides=(1,), padding=[(K - 1, 0)], dimension_numbers=('NHC', 'HIO', 'NHC'), feature_group_count=C)
        return y

    def _L3_cond_ref(x, w, b):
        import jax, jax.numpy as jnp
        import numpy as np
        'Depthwise causal conv1d, channel-last.\n            x: (B, L, D); w: (K, 1, D); b: (D,). Returns (B, L, D).\n            Matches torch: Conv1d(D, D, K, groups=D, padding=K-1)(x.T)[..., :L].T\n            which is exactly a causal conv (left pad K-1, trim to L).\n            '
        K = w.shape[0]
        D = x.shape[-1]
        y = jax.lax.conv_general_dilated(x, w, window_strides=(1,), padding=[(K - 1, 0)], feature_group_count=D, dimension_numbers=('NWC', 'WIO', 'NWC'))
        return y + b
    x = x + _L0_cond_ref(x, cond_2048[:, None, :], L0_cond_W_emb, L0_cond_b_emb, L0_cond_g_norm, L0_cond_W_qkv, L0_cond_g_q, L0_cond_g_k, L0_cond_W_out)
    x = x + _L1_cond_ref(cond_2048, x, L1_cond_W_ih, L1_cond_W_hh, L1_cond_b_ih, L1_cond_b_hh)
    x = x + _L2_cond_ref(x, cond_2048[:, None, :])
    x = x + _L3_cond_ref(x, cond_2048[:, None, :], L3_cond_b)
    return x

_drawn_inputs = setup_inputs


def setup_inputs(seed=0):
    import zlib

    import numpy as np

    out = dict(_drawn_inputs(seed))
    spreads = {'L0_cond_b_emb': (0.0, 0.1),
     'L0_cond_g_norm': (1.0, 0.2),
     'L0_cond_g_q': (1.0, 0.6),
     'L0_cond_g_k': (1.0, 0.6),
     'L1_cond_b_ih': (0.0, 0.329),
     'L1_cond_b_hh': (0.0, 0.53)}
    factors = {'L3_cond_b': 8.0}
    for name, (base, spread) in spreads.items():
        noise = np.random.default_rng([zlib.crc32(name.encode()), seed]).standard_normal(out[name].shape)
        drawn = base * np.exp(spread * noise) if base else spread * noise
        out[name] = jnp.asarray(drawn.astype(out[name].dtype))
    for name, factor in factors.items():
        out[name] = (out[name] * factor).astype(out[name].dtype)
    return out
```

```python
import concourse.bass as bass
from concourse import mybir
from contextlib import ExitStack

F32 = mybir.dt.float32
ALU = mybir.AluOpType
ACT = mybir.ActivationFunctionType
AX = mybir.AxisListType

B, T, D, HEADS = 4, 512, 512, 16
P = 128
C = D // P
NG = 4
DH = D // HEADS
TAPS = B
PAD = TAPS - 1
TP = T + PAD
TB = T // P
NI = C * B
EPS = 1e-6


R_COND, R_GN, R_B3, R_BES, R_BEH, R_BI, R_BH, R_GQ, R_GK = 0, 4, 5, 6, 7, 8, 11, 14, 15


class Queue:

    def __init__(self, sem):
        self.sem, self.items, self.at = sem, [], {}

    def add(self, name, waits, fn):
        assert name not in self.at, name
        self.items.append((name, waits, fn))
        self.at[name] = len(self.items)

    def run(self, eng, passes, apart=None):
        dma = isinstance(self.sem, list)
        for sem in self.sem if dma else [self.sem]:
            eng.sem_inc(sem, 16 if dma else len(self.items))
        with eng.Fori(0, passes) as it:
            passed = {}
            for i, (name, waits, fn) in enumerate(self.items):
                for w in waits:
                    q, other, before = w if len(w) == 3 else (*w, False)
                    n, total = q.at[other], len(q.items)
                    if isinstance(q.sem, list):
                        sem, value = q.sem[n - 1], (it + (1 if before else 2)) * 16
                    else:
                        if before:
                            n -= total
                        if passed.get(id(q), -total) >= n:
                            continue
                        passed[id(q)] = n
                        sem, value = q.sem, it * total + (total + n)
                    eng.wait_ge(sem, value)
                    if apart is not None:
                        eng.sem_inc(apart, 1)
                fn(eng, it).then_inc(self.sem[i] if dma else self.sem, 16 if dma else 1)


def regroup(src, dst):
    return (src.rearrange("p (g c j) -> p c g j", g=NG, c=C), dst.rearrange("p (c g j) -> p c g j", g=NG, c=C))


def load_rows(eng, dst, src, sem):
    rows = src.rearrange("(g c j) n -> g j c n", g=NG, c=C)
    for g in range(NG):
        eng.dma_start(dst[32 * g:32 * g + 32], rows[g]).then_inc(sem, 16)


def build(nc, x, cond, W_emb, b_emb, g_norm, W_qkv, g_q, g_k, W_out, W_ih, W_hh, b_ih, b_hh, b3, out):
    with ExitStack() as ctx:
        def sb(name, shape):
            return ctx.enter_context(nc.sbuf_tensor(name, shape, F32))

        def sem(name):
            return ctx.enter_context(nc.semaphore(name))

        bank = [ctx.enter_context(nc.psum_tensor(f"bank{i}", [P, 512], F32)) for i in range(8)]

        whh = sb("whh", [P, C, 3 * D])
        seq = sb("seq", [P, NI, TP])
        ident = sb("ident", [P, P])
        vecT = sb("vecT", [P, C, 32])
        bias_g = sb("bias_g", [P, 3, C])
        tap = sb("tap", [P, TAPS, NI, 2])
        b3x = sb("b3x", [P, NI, 2])
        arena = sb("arena", [P, 48 * T])
        arena2 = sb("arena2", [P, NI * TP])
        gi = arena[:].rearrange("p (t i) -> p t i", i=48)
        seq2 = arena2[:].rearrange("p (i t) -> p i t", i=NI)
        wih = arena2[:, 0:C * 3 * D].rearrange("p (c n) -> p c n", c=C)

        at = [0]

        def take(n):
            at[0] += n
            assert at[0] <= 48 * T
            return arena[:, at[0] - n:at[0]]

        wqkv = take(C * 3 * D).rearrange("p (c n) -> p c n", c=C)
        wout = take(C * D).rearrange("p (c n) -> p c n", c=C)
        x_nat = take(TB * D).rearrange("p (t n) -> p t n", t=TB)
        xp = take(TB * D).rearrange("p (t n) -> p t n", t=TB)
        xnT = take(C * T).rearrange("p (c t) -> p c t", c=C)
        v_nat = take(TB * D).rearrange("p (t n) -> p t n", t=TB)
        oT = take(C * T).rearrange("p (c t) -> p c t", c=C)
        kT = take(2 * T).rearrange("p (a t) -> p a t", a=2)
        qm = take(2 * NG * T).rearrange("p (a g t) -> p a g t", a=2, g=NG)
        qn = take(T)
        sqb = take(T)
        wemb = arena2[:, 0:C * 2 * D].rearrange("p (c n) -> p c n", c=C)
        stage = oT[:, 0, 0:P]
        rnb = sb("rnb", [P, T])
        pT = arena2[:, 0:NG * TB * T].rearrange("p (g b n) -> p g b n", g=NG, b=TB)
        NP = 8
        prob = sb("prob", [P, NP, T])
        small = sb("small", [P, 64])
        mn, sm, ri = small[:, 0:8], small[:, 8:16], small[:, 16:24]
        ssx, lnx, rsx = small[:, 24:28], small[:, 28:32], small[:, 32:36]
        cur = small[:, 36:44].rearrange("p (s c) -> p s c", s=2)
        eps = small[:, 44:45]
        maskn = small[:, 45:49]
        modT = sb("modT", [P, 2, C, B])
        ones = sb("ones", [P, P])

        s_const = sem("s_const")
        s_id = sem("s_id")
        s_wl = sem("s_wl")
        s_vec = sem("s_vec")
        s_emb = sem("s_emb")
        s_mod = sem("s_mod")
        s_modT = sem("s_modT")
        s_wkv = sem("s_wkv")
        s_wout = sem("s_wout")
        n_vec = 4 * 11 + 2 * NG
        with nc.Block() as block:
            @block.sync
            def _(e):
                e.wait_ge(s_const, 1)
                for g in range(NG):
                    cols = slice(128 * g, 128 * g + 128)
                    e.dma_start(stage[32 * g:32 * g + B, :], cond[:, cols]).then_inc(s_vec, 16)
                    rows = [(R_GN, g_norm[cols]), (R_B3, b3[cols]), (R_BES, b_emb[cols]),
                            (R_BEH, b_emb[D + 128 * g:D + 128 * g + 128])]
                    rows += [(R_BI + q, b_ih[q * D + 128 * g:q * D + 128 * g + 128]) for q in range(3)]
                    rows += [(R_BH + q, b_hh[q * D + 128 * g:q * D + 128 * g + 128]) for q in range(3)]
                    for r, v in rows:
                        e.dma_start(stage[32 * g + r:32 * g + r + 1, :],
                                    v.rearrange("(a n) -> a n", a=1)).then_inc(s_vec, 16)
                    for r, v in ((R_GQ, g_q), (R_GK, g_k)):
                        e.dma_start(stage[32 * g + r:32 * g + r + 1, 0:DH],
                                    v.rearrange("(a n) -> a n", a=1)).then_inc(s_vec, 16)

            @block.scalar
            def _(e):
                load_rows(e, wemb, W_emb, s_emb)
                load_rows(e, whh[:], W_qkv, s_wkv)
                load_rows(e, x_nat, W_out, s_wout)
                e.wait_ge(s_wkv, NG * 16)
                for i in range(3 * C):
                    if i % 2 == 0:
                        a, b = regroup(whh[:, i // 3, i % 3 * D:i % 3 * D + D], wqkv[:, i // 3, i % 3 * D:i % 3 * D + D])
                        e.activation(b, a, ACT.Copy)

            @block.gpsimd
            def _(e):
                e.memset(ident[:], 0.0).then_inc(s_id, 1)
                e.wait_ge(s_id, 1)
                e.affine_select(out=ident[:], in_=ident[:], compare_op=ALU.not_equal, fill=1.0, base=0,
                                pattern=[[-1, P]], channel_multiplier=1).then_inc(s_id, 1)
                e.memset(seq[:, :, 0:PAD], 0.0).then_inc(s_id, 1)

            @block.vector
            def _(e):
                e.memset(stage, 0.0).then_inc(s_const, 1)
                e.memset(bank[0][:], 0.0).then_inc(s_const, 1)
                e.memset(ones[:], 0.0).then_inc(s_const, 1)
                e.memset(maskn, 0.0).then_inc(s_const, 1)
                e.memset(eps, EPS).then_inc(s_const, 1)
                e.wait_ge(s_const, 5)
                for g in range(NG):
                    q = slice(32 * g, 32 * g + 32)
                    e.memset(ones[q, q], 1.0).then_inc(s_const, 1)
                    e.memset(maskn[q, g:g + 1], -float(DH) ** -0.5).then_inc(s_const, 1)
                e.wait_ge(s_vec, n_vec * 16 // 1)
                e.transpose(vecT[:], stage.rearrange("p (c i) -> p c i", c=C)).then_inc(s_mod, 1)
                e.wait_ge(s_mod, 1)
                for q in range(2):
                    e.tensor_tensor(bias_g[:, q, :], vecT[:, :, R_BI + q], vecT[:, :, R_BH + q],
                                    ALU.add).then_inc(s_mod, 1)
                e.tensor_copy(bias_g[:, 2, :], vecT[:, :, R_BI + 2]).then_inc(s_mod, 1)
                for h in range(2):
                    for b in range(B):
                        for s in range(2):
                            i = (h * B + b) * 2
                            e.tensor_copy(tap[:, :, i:i + 2, s],
                                          vecT[:, 2 * h:2 * h + 2, 0:TAPS].rearrange("p c k -> p k c"))
                            e.tensor_copy(b3x[:, i:i + 2, s], vecT[:, 2 * h:2 * h + 2, R_B3]).then_inc(s_mod, 1)
                e.wait_ge(s_wkv, NG * 16)
                for i in range(3 * C):
                    if i % 2:
                        a, b = regroup(whh[:, i // 3, i % 3 * D:i % 3 * D + D], wqkv[:, i // 3, i % 3 * D:i % 3 * D + D])
                        e.tensor_copy(b, a)
                e.wait_ge(s_wout, NG * 16)
                for k in range(C):
                    a, b = regroup(x_nat[:, k, :], wout[:, k, :])
                    e.tensor_copy(b, a)
                e.wait_ge(s_modT, 1)
                sT = xp[:, 0, 0:256].rearrange("p (q c i) -> p q c i", q=2, c=C)
                e.transpose(sT, bank[0][:, 0:256].rearrange("p (q c i) -> p q c i", q=2, c=C)).then_inc(s_modT, 1)
                e.wait_ge(s_modT, 2)
                for c in range(C):
                    e.tensor_scalar(modT[:, 0, c, :], sT[:, 0, c, 0:B], vecT[:, c, R_BES:R_BES + 1], 1.0,
                                    ALU.add, ALU.add).then_inc(s_modT, 1)
                    e.tensor_scalar(modT[:, 1, c, :], sT[:, 1, c, 0:B], vecT[:, c, R_BEH:R_BEH + 1], None,
                                    ALU.add).then_inc(s_modT, 1)
                e.wait_ge(s_modT, 2 + 2 * C)
                for c in range(C):
                    e.tensor_scalar(modT[:, 0, c, :], modT[:, 0, c, :], vecT[:, c, R_GN:R_GN + 1], None,
                                    ALU.mult).then_inc(s_modT, 1)

            @block.tensor
            def _(e):
                e.wait_ge(s_emb, NG * 16)
                e.wait_ge(s_const, 2)
                e.wait_ge(s_mod, 1)
                wv = wemb.rearrange("p c (q G n) -> p c q G n", q=2, G=NG)
                for k in range(C):
                    for G in range(NG):
                        last = e.matmul(bank[0][32 * G:32 * G + B, 0:256], vecT[:, k, 0:B], wv[:, k, :, G, :],
                                        start=k == 0, stop=k == C - 1)
                last.then_inc(s_modT, 1)

        qs_, qa, qv, qg, qp = (Queue([sem("l0_load")]), Queue(sem("l0_act")), Queue(sem("l0_dve")),
                               Queue(sem("l0_pool")), Queue(sem("l0_pe")))
        xv = x.rearrange("b (t p) n -> b p t n", p=P)
        qs_.add("x", [(qa, "xp3", True)],
                lambda e, b: e.dma_start(x_nat, xv[bass.ds(b, 1)].rearrange("a p t n -> p (a t) n")))

        def halves(view, b):
            return view

        seq5 = seq[:].rearrange("p (h b c) t -> p h b c t", h=2, b=B)

        def seq_at(c, b):
            return seq5[:, c // 2, bass.ds(b, 1), c % 2, PAD:TP]

        for t in range(TB):
            qa.add(f"sq{t}", [(qs_, "x"), (qp, "ks3", True)] + [(qa, f"sq{t - 1}")] * (t > 0),
                   lambda e, b, t=t: e.activation(sqb, x_nat[:, t, :], ACT.Square, accum_out=ssx[:, t:t + 1]))

        def group(e, t):
            a, b = regroup(x_nat[:, t, :], xp[:, t, :])
            return e.activation(b, a, ACT.Copy)
        for t in range(TB):
            qa.add(f"xp{t}", [(qg, "o23", True)], lambda e, b, t=t: group(e, t))
        qa.add("lnx", [(qa, "sq3")], lambda e, b: e.activation(lnx, ssx, ACT.Ln, bias=eps, scale=1.0 / D))
        qa.add("rsx", [(qa, "lnx")], lambda e, b: e.activation(rsx, lnx, ACT.Exp, scale=-0.5))
        qv.add("cur", [], lambda e, b: e.tensor_copy(cur, modT[:].rearrange("p s c b -> p (s c) b")[:, :, bass.ds(b, 1)]
                                                    .rearrange("p (s c) b -> p s (c b)", s=2)))
        for t in range(TB):
            qv.add(f"xn{t}", [(qa, "rsx"), (qp, "tx3")],
                   lambda e, b, t=t: e.tensor_scalar(xp[:, t, :], xp[:, t, :], rsx[:, t:t + 1], None, ALU.mult))

        def transposes(e, dst, src, c):
            for t in range(TB):
                last = e.transpose(dst[:, 128 * t:128 * t + 128],
                                   src[:, t, 128 * c:128 * c + 128], ident[:])
            return last

        for c in range(C):
            qp.add(f"tx{c}", [(qa, "xp3"), (qv, "o13", True)],
                   lambda e, b, c=c: transposes(e, bank[c], xp, c))
            qa.add(f"xr{c}", [(qp, f"tx{c}")],
                   lambda e, b, c=c: e.activation(seq_at(c, b), bank[c][:].rearrange("p (a t) -> p a t", a=1), ACT.Copy))
        for c in range(C):
            qp.add(f"tn{c}", [(qv, "xn3")], lambda e, b, c=c: transposes(e, bank[4 + c], xp, c))
            qv.add(f"xt{c}", [(qp, f"tn{c}"), (qp, "k3", True), (qv, "cur")],
                   lambda e, b, c=c: e.tensor_scalar(xnT[:, c, :], bank[4 + c][:], cur[:, 0, c:c + 1],
                                                     cur[:, 1, c:c + 1], ALU.mult, ALU.add))

        def vproj(e, b, t):
            for k in range(C):
                last = e.matmul(bank[t][:], xnT[:, k, 128 * t:128 * t + 128], wqkv[:, k, 2 * D:3 * D],
                                start=k == 0, stop=k == C - 1)
            return last
        for t in range(TB):
            qp.add(f"v{t}", [(qv, "xt3"), (qa, f"xr{t}")], lambda e, b, t=t: vproj(e, b, t))
            qa.add(f"ve{t}", [(qp, f"v{t}"), (qp, "pv3", True)],
                   lambda e, b, t=t: e.activation(v_nat[:, t, :], bank[t][:], ACT.Copy))

        QK, SS, OB = 5, 6, 7
        wq = wqkv.rearrange("p k (s c n) -> p k s c n", s=3, c=C)

        def proj(e, b, s, c):
            for k in range(C):
                last = e.matmul(bank[QK][:], wq[:, k, s, c], xnT[:, k, :], start=k == 0, stop=k == C - 1)
            return last

        def norm_start(s, c):
            n = "qk"[s]
            prior = (qv, "xt3") if (s, c) == (0, 0) else (qv, f"qn{c}" if s else f"kn{c - 1}")
            qp.add(f"{n}{c}", [prior, (qv, "xt3")], lambda e, b: proj(e, b, s, c))
            qa.add(f"{n}2{c}", [(qp, f"{n}{c}"), (qp, f"{'q' if s else 'k'}s{c if s else c - 1}")
                                if (s, c) != (0, 0) else (qa, "sq3")],
                   lambda e, b: e.activation(sqb, bank[QK][:], ACT.Square))

        def norm_end(s, c):
            n = "qk"[s]
            qp.add(f"{n}s{c}", [(qa, f"{n}2{c}"), (qv, "xt3")],
                   lambda e, b: e.matmul(bank[SS][:], ones[:], sqb, start=True, stop=True))
            qa.add(f"{n}l{c}", [(qp, f"{n}s{c}"), (qv, f"qn{c}") if s else
                                ((qv, f"kn{c - 1}") if c else (qv, "kn3", True))],
                   lambda e, b: e.activation(rnb[:], bank[SS][:], ACT.Ln, bias=eps, scale=1.0 / DH))
            qa.add(f"{n}r{c}", [(qa, f"{n}l{c}")],
                   lambda e, b: e.activation(rnb[:], rnb[:], ACT.Exp, scale=-0.5))
            if s == 0:
                qv.add(f"qn{c}", [(qa, f"qr{c}"), (qg, f"qm{c - 1}3") if c else (qg, "qm33", True)],
                       lambda e, b: e.scalar_tensor_tensor(qn, bank[QK][:], vecT[:, 0, R_GQ:R_GQ + 1], rnb[:],
                                                           ALU.mult, ALU.mult))
                for g in range(NG):
                    free = (qp, f"S{16 * (c - 2) + 15}") if c >= 2 else (qp, f"S{16 * (c + 2) + 15}", True)
                    qg.add(f"qm{c}{g}", [(qv, f"qn{c}"), free],
                           lambda e, b, g=g: e.tensor_scalar(qm[:, c % 2, g, :], qn, maskn[:, g:g + 1], 1.0,
                                                             ALU.mult, ALU.mult))
            else:
                free = (qp, f"S{16 * (c - 2) + 15}") if c >= 2 else (qp, f"S{16 * (c + 2) + 15}", True)
                qv.add(f"kn{c}", [(qa, f"kr{c}"), free],
                       lambda e, b: e.scalar_tensor_tensor(kT[:, c % 2, :], bank[QK][:], vecT[:, 0, R_GK:R_GK + 1],
                                                           rnb[:], ALU.mult, ALU.mult))

        NS = 3
        LAG = 3

        def products(m):
            c, g, t = m // 16, m // 4 % 4, m % 4
            if m == 0:
                free = (qa, "ve2")
            elif m < NS:
                free = (qa, "ve2")
            else:
                free = (qa, f"e{m - NS}")
            qp.add(f"S{m}", [(qg, f"qm{c}3"), (qv, f"kn{c}"), free],
                   lambda e, b: e.matmul(bank[m % NS][:], qm[:, c % 2, g, 128 * t:128 * t + 128], kT[:, c % 2, :],
                                         start=True, stop=True))
            r = slice(m % NP, m % NP + 1)
            qv.add(f"mn{m}", [(qp, f"S{m}"), (qa, f"e{m - NP}") if m >= NP else (qa, f"e{64 + m - NP}", True)],
                   lambda e, b: e.tensor_reduce(mn[:, r], bank[m % NS][:], AX.X, ALU.min))
            qa.add(f"e{m}", [(qv, f"mn{m}"), (qp, f"T{m - NP}") if m >= NP else (qp, f"T{64 + m - NP}", True),
                             (qv, f"ri{m - NP}") if m >= NP else (qv, f"ri{64 + m - NP}", True)],
                   lambda e, b: e.activation(prob[:, m % NP, :], bank[m % NS][:], ACT.Exp, bias=mn[:, r], scale=-1.0,
                                             accum_out=sm[:, r]))
            qv.add(f"ri{m}", [(qa, f"e{m}"), (qg, f"n{m - NP}") if m >= NP else (qg, f"n{64 + m - NP}", True)],
                   lambda e, b: e.reciprocal(ri[:, r], sm[:, r]))
            qg.add(f"n{m}", [(qv, f"ri{m}")],
                   lambda e, b: e.tensor_scalar(prob[:, m % NP, :], prob[:, m % NP, :], ri[:, r], 1.0,
                                                ALU.mult, ALU.mult))

        def turn(m):
            c, g, t = m // 16, m // 4 % 4, m % 4
            dst = bank[3 + m % 2]

            def tr(e, b):
                for k in range(TB):
                    last = e.transpose(dst[:, 128 * k:128 * k + 128], prob[:, m % NP, 128 * k:128 * k + 128], ident[:])
                return last
            qe = (qa, qv)[m % 2]
            prior = (qe, f"p{m - 2}") if m >= 2 else ((qa, "ve3") if m == 0 else (qv, "xt3"))
            qp.add(f"T{m}", [(qg, f"n{m}"), prior], tr)
            free = (qp, f"pv{c - 1}") if c else (qp, "pv3", True)
            if m % 2 == 0:
                qa.add(f"p{m}", [(qp, f"T{m}"), free], lambda e, b: e.activation(pT[:, g, t, :], dst[:], ACT.Copy))
            else:
                qv.add(f"p{m}", [(qp, f"T{m}"), free], lambda e, b: e.tensor_copy(pT[:, g, t, :], dst[:]))

        def values(c):
            def pv(e, b):
                for k in range(TB):
                    for g in range(NG):
                        last = e.matmul(bank[OB][32 * g:32 * g + DH, :],
                                        v_nat[:, k, 128 * c + 32 * g:128 * c + 32 * g + DH],
                                        pT[:, g, :, 128 * k:128 * k + 128], start=k == 0, stop=k == TB - 1)
                return last
            qp.add(f"pv{c}", [(qa, f"p{16 * c + 14}"), (qv, f"p{16 * c + 15}"), (qa, f"ve3"),
                              (qa, f"oe{c - 1}") if c else (qv, "xt3")], pv)
            qa.add(f"oe{c}", [(qp, f"pv{c}"), (qv, "o13", True)],
                   lambda e, b: e.activation(oT[:, c, :], bank[OB][:], ACT.Copy))

        norm_start(0, 0)
        norm_end(0, 0)
        norm_start(1, 0)
        norm_end(1, 0)
        for m in range(64 + LAG + 1):
            if m < 64:
                products(m)
                if m // 16 < 3:
                    c1 = m // 16 + 1
                    {1: lambda: norm_start(0, c1), 4: lambda: norm_end(0, c1),
                     7: lambda: norm_start(1, c1), 10: lambda: norm_end(1, c1)}.get(m % 16, lambda: None)()
            if m >= 19 and m % 16 == LAG:
                values(m // 16 - 1)
            if LAG <= m < 64 + LAG:
                turn(m - LAG)
        wo = wout.rearrange("p k (c n) -> p k c n", c=C)
        OBANK = [5, 6, 0, 1]

        def oproj(e, b, c):
            for k in range(C):
                last = e.matmul(bank[OBANK[c]][:], wo[:, k, c], oT[:, k, :], start=k == 0, stop=k == C - 1)
            return last
        for c in range(C):
            qp.add(f"op{c}", [(qa, "oe3"), (qa, "e63"), (qv, "kn3")], lambda e, b, c=c: oproj(e, b, c))
            tmp = xp[:, c, :]
            qv.add(f"o1{c}", [(qp, f"op{c}"), (qg, f"o2{c}", True)],
                   lambda e, b, c=c, tmp=tmp: e.tensor_tensor(tmp, bank[OBANK[c]][:], oT[:, c, :], ALU.add))
            qg.add(f"o2{c}", [(qv, f"o1{c}"), (qa, f"xr{c}")],
                   lambda e, b, c=c, tmp=tmp: e.tensor_tensor(seq_at(c, b), seq_at(c, b),
                                                              tmp.rearrange("p (a t) -> p a t", a=1), ALU.add))
        s_wih = sem("s_wih")
        s_whh = sem("s_whh")
        s_reg = sem("s_reg")
        s_apart = sem("s_apart")
        with nc.Block() as block:
            @block.sync
            def _(e):
                load_rows(e, whh[:], W_hh, s_whh)
                qs_.run(e, B)
                e.wait_ge(qp.sem, B * len(qp.items) + qp.at["k3"])
                load_rows(e, wqkv, W_ih, s_wih)
                e.wait_ge(s_whh, NG * 16)
                e.wait_ge(s_wih, NG * 16)

            @block.scalar
            def _(e):
                qa.run(e, B)

            @block.vector
            def _(e):
                qv.run(e, B)

            @block.gpsimd
            def _(e):
                qg.run(e, B, apart=s_apart)

            @block.tensor
            def _(e):
                qp.run(e, B)

        ga, gv, gp = Queue(sem("gi_act")), Queue(sem("gi_dve")), Queue(sem("gi_pe"))
        wi = wih.rearrange("p k (q c n) -> p k q c n", q=3, c=C)
        gi6 = arena[:].rearrange("p (t q h b c) -> p t q h b c", q=3, h=2, b=B, c=2)
        for i in range(3 * C):
            q, c = i // C, i % C

            def prod(e, b, i=i, q=q, c=c):
                for k in range(C):
                    last = e.matmul(bank[i % 6][:], wi[:, k, q, c], seq_at(k, b), start=k == 0, stop=k == C - 1)
                return last
            qe = (ga, gv)[i % 2]
            gp.add(f"g{i}", [(qe, f"g{i - 6}") if i >= 6 else (qe, f"g{i + 6}", True)], prod)
            dst = gi6[:, :, q, c // 2, :, c % 2]
            if i % 2 == 0:
                ga.add(f"g{i}", [(gp, f"g{i}")], lambda e, b, i=i, q=q, c=c, dst=dst: e.activation(
                    dst[:, :, bass.ds(b, 1)], bank[i % 6][:].rearrange("p (t a) -> p t a", a=1), ACT.Identity,
                    bias=bias_g[:, q, c:c + 1]))
            else:
                gv.add(f"g{i}", [(gp, f"g{i}")], lambda e, b, i=i, q=q, c=c, dst=dst: e.tensor_scalar(
                    dst[:, :, bass.ds(b, 1)], bank[i % 6][:].rearrange("p (t a) -> p t a", a=1),
                    bias_g[:, q, c:c + 1], None, ALU.add))
        with nc.Block() as block:
            def regroup_ih(e, first, copy):
                for i in range(first, 3 * C, 2):
                    a, b = regroup(wqkv[:, i // 3, i % 3 * D:i % 3 * D + D], wih[:, i // 3, i % 3 * D:i % 3 * D + D])
                    copy(b, a).then_inc(s_reg, 1)
                e.wait_ge(s_reg, 3 * C)

            @block.tensor
            def _(e):
                e.wait_ge(s_reg, 3 * C)
                gp.run(e, B)

            @block.scalar
            def _(e):
                regroup_ih(e, 0, lambda b, a: e.activation(b, a, ACT.Copy))
                ga.run(e, B)

            @block.vector
            def _(e):
                regroup_ih(e, 1, lambda b, a: e.tensor_copy(b, a))
                gv.run(e, B)

        used = [0]
        prob_flat = prob[:].rearrange("p a t -> p (a t)")

        def tile(shape):
            n = 1
            for d in shape[1:]:
                n *= d
            used[0] += n
            assert used[0] <= NP * T
            v = prob_flat[:, used[0] - n:used[0]]
            return v if len(shape) == 2 else v.rearrange("p (a b) -> p a b", a=shape[1])

        hb = tile([P, 2, 4 * NI])
        tr_rz = tile([P, 2, P])
        s_rz_ = tile([P, 2 * NI])
        gin = tile([P, 2, 2 * NI])
        r_d0 = tile([P, 2 * NI])
        n_d1 = tile([P, 2, P])
        scA = tile([P, 2 * NI])
        m_d0 = tile([P, 4 * NI])
        z_d1 = tile([P, 4 * NI])
        brow = tile([P, NG, P])
        row0 = tile([P, B])
        prd = tile([P, 2, TAPS * NI * 2])
        st = {n: sem(n) for n in ("s_clear", "s_brow", "s_h", "s_rz", "s_n", "s_tr", "s_sum", "s_sig", "s_pre", "s_gi",
                                  "s_tanh", "s_hold", "s_x3", "s_pool")}
        RZ, BN = 0, ((1, 2), (3, 4))

        def every(ap, n):
            return ap.rearrange("p (i s) -> p i s", s=n)

        N_CLEAR = 14
        with nc.Block() as block:
            @block.sync
            def _(e):
                e.wait_ge(st["s_clear"], 1)
                e.dma_start(brow[0:1], b_hh[2 * D:3 * D].rearrange("(a g n) -> a g n", a=1, g=NG)).then_inc(st["s_brow"], 16)
                e.wait_ge(st["s_brow"], 16)

            @block.vector
            def _(e):
                c = st["s_clear"]
                e.memset(brow[:], 0.0).then_inc(c, 1)
                for v in (row0[:], r_d0[:], m_d0[:], n_d1[:], bank[RZ][:], bank[1][:], bank[2][:], bank[3][:],
                          bank[4][:], seq2[:, :, 0:PAD]):
                    e.memset(v, 0.0).then_inc(c, 1)
                e.memset(z_d1[:], -1.0).then_inc(c, 1)
                e.wait_ge(c, 12)
                e.memset(row0[0:1, :], 1.0).then_inc(c, 1)
                e.memset(every(z_d1[:], 4)[:, :, 0], 0.0).then_inc(c, 1)
                e.wait_ge(c, N_CLEAR)
                with e.Fori(0, T // 2) as it:
                    for u in range(2):
                        t = it * 2 + u
                        t1, h1, h2 = e.snap(t + 1), e.snap(2 * t + 1), e.snap(2 * t + 2)
                        t4 = [e.snap(4 * t + i) for i in (1, 2, 3, 4)]
                        h4 = e.snap(2 * t + 4)
                        now = e.snap(t + PAD)

                        def turn_rz(q):
                            e.transpose(tr_rz[:, q, :].rearrange("p (h i c) -> p h c i", c=2, h=2),
                                        bank[RZ][:, P * q:P * q + P].rearrange("p (h c i) -> p h c i", h=2, c=2)
                                        ).then_inc(st["s_tr"], 1)

                        def add_gi(q):
                            s = slice(NI * q, NI * q + NI)
                            e.tensor_tensor(s_rz_[:, s].rearrange("p (h i) -> p h i", h=2),
                                            tr_rz[:, q, :].rearrange("p (h i) -> p h i", h=2)[:, :, 0:8],
                                            gin[:, u, s].rearrange("p (h i) -> p h i", h=2),
                                            ALU.add).then_inc(st["s_sum"], 1)

                        def turn_n(h):
                            e.wait_ge(st["s_n"], (h1, h2)[h])
                            e.transpose(n_d1[:, h, :].rearrange("p (i c s) -> p c i s", c=2, s=2)[:, :, :, 0],
                                        bank[BN[h][u]][:, 0:64].rearrange("p (c i) -> p c i", c=2)
                                        ).then_inc(st["s_tr"], 1)

                        def scan_a(h):
                            s = slice(NI * h, NI * h + NI)
                            e.tensor_tensor_scan(scA[:, s], r_d0[:, s], n_d1[:, h, 0:NI], 0.0, ALU.mult, ALU.add
                                                 ).then_inc(st["s_pre"], 1)

                        def scan_b(h):
                            e.wait_ge(st["s_tanh"], (h1, h2)[h])
                            s = slice(2 * NI * h, 2 * NI * h + 2 * NI)
                            e.tensor_tensor_scan(hb[:, 1 - u, s], m_d0[:, s], z_d1[:, s], 0.0, ALU.subtract, ALU.mult
                                                 ).then_inc(st["s_h"], 1)

                        e.wait_ge(st["s_gi"], t1)
                        e.wait_ge(st["s_rz"], t1)
                        turn_rz(0)
                        e.wait_ge(st["s_tr"], t4[0])
                        add_gi(0)
                        turn_rz(1)
                        turn_n(0)
                        e.wait_ge(st["s_tr"], t4[1])
                        add_gi(1)
                        e.wait_ge(st["s_tr"], t4[2])
                        e.wait_ge(st["s_sig"], h1)
                        scan_a(0)
                        scan_b(0)
                        turn_n(1)
                        e.wait_ge(st["s_tr"], t4[3])
                        scan_a(1)
                        scan_b(1)
                        e.wait_ge(st["s_h"], h4)
                        e.tensor_tensor(seq[:, :, bass.ds(now, 1)], seq[:, :, bass.ds(now, 1)],
                                        every(hb[:, 1 - u, :], 4)[:, :, 3:4], ALU.add).then_inc(st["s_x3"], 1)

            @block.scalar
            def _(e):
                e.wait_ge(st["s_clear"], N_CLEAR)
                e.preload_act_table_set("sigmoid_and_others")
                n_in = n_d1[:, :, 0:NI].rearrange("p h (i s) -> p h i s", s=2)[:, :, :, 1]

                def bring(t, u):
                    e.activation(gin[:, u:u + 1, :], gi[:, bass.ds(t, 1), 0:2 * NI], ACT.Copy)
                    e.activation(n_in, gi[:, bass.ds(t, 1), 2 * NI:3 * NI].rearrange("p a (h i) -> p (a h) i", h=2),
                                 ACT.Copy).then_inc(st["s_gi"], 1)
                for h in range(2):
                    src = vecT[:, 2 * h:2 * h + 2, 0:B].rearrange("p c b -> p b c")
                    s = slice(2 * NI * h, 2 * NI * h + 2 * NI)
                    e.activation(hb[:, 0, s].rearrange("p (b c s) -> p b c s", b=B, c=2)[:, :, :, 3], src, ACT.Copy)
                    e.activation(m_d0[:, s].rearrange("p (b c s) -> p b c s", b=B, c=2)[:, :, :, 2], src,
                                 ACT.Copy).then_inc(st["s_h"], 1)
                with e.Fori(0, T // 2) as it:
                    for u in range(2):
                        t = it * 2 + u
                        h1, h2, h4 = e.snap(2 * t + 1), e.snap(2 * t + 2), e.snap(2 * t + 4)
                        bring(e.snap(t), u)
                        e.wait_ge(st["s_sum"], h1)
                        e.activation(every(r_d0[:], 2)[:, :, 1], s_rz_[:, 0:NI], ACT.Sigmoid).then_inc(st["s_sig"], 1)
                        e.wait_ge(st["s_sum"], h2)
                        e.activation(every(z_d1[:], 4)[:, :, 2], s_rz_[:, NI:2 * NI], ACT.Sigmoid).then_inc(st["s_sig"], 1)
                        for h in range(2):
                            e.wait_ge(st["s_pre"], (h1, h2)[h])
                            pre = every(scA[:, NI * h:NI * h + NI], 2)[:, :, 1:2]
                            dst = m_d0[:, 2 * NI * h:2 * NI * h + 2 * NI].rearrange("p (i a s) -> p i a s", a=2, s=2)
                            e.activation(dst[:, :, :, 1], pre.broadcast_to([P, 8, 2]), ACT.Tanh, scale=-1.0
                                         ).then_inc(st["s_tanh"], 1)
                        e.wait_ge(st["s_h"], h4)
                        e.activation(every(m_d0[:], 4)[:, :, 2], every(hb[:, 1 - u, :], 4)[:, :, 3], ACT.Copy)

            @block.tensor
            def _(e):
                e.wait_ge(st["s_clear"], N_CLEAR)
                e.wait_ge(st["s_brow"], 16)

                def bias(u):
                    for h in range(2):
                        for G in range(NG):
                            e.matmul(bank[BN[h][u]][32 * G:32 * G + B, 0:64], row0[:], brow[:, G, 64 * h:64 * h + 64],
                                     start=True, stop=False)
                bias(0)
                wv = whh[:].rearrange("p c (q G n) -> p c q G n", q=3, G=NG)
                with e.Fori(0, T // 2) as it:
                    for u in range(2):
                        t = it * 2 + u
                        h1, h2 = e.snap(2 * t + 1), e.snap(2 * t + 2)
                        hv = hb[:, u, :].rearrange("p (h b c s) -> p h b c s", h=2, c=2, s=4)
                        for k in range(C):
                            if k % 2 == 0:
                                e.wait_ge(st["s_h"], (h1, h2)[k // 2])
                            for G in range(NG):
                                last = e.matmul(bank[RZ][32 * G:32 * G + B, 0:2 * P], hv[:, k // 2, :, k % 2, 3],
                                                wv[:, k, 0:2, G, :], start=k == 0, stop=k == C - 1)
                        last.then_inc(st["s_rz"], 1)
                        for h in range(2):
                            for k in range(C):
                                for G in range(NG):
                                    last = e.matmul(bank[BN[h][u]][32 * G:32 * G + B, 0:64],
                                                    hv[:, k // 2, :, k % 2, 3],
                                                    wv[:, k, 2, G, 64 * h:64 * h + 64], start=False, stop=k == C - 1)
                            last.then_inc(st["s_n"], 1)
                        bias(1 - u)

            @block.gpsimd
            def _(e):
                e.wait_ge(st["s_clear"], N_CLEAR)
                s = st["s_pool"]

                def wait(sem_, n):
                    e.wait_ge(sem_, n)
                    e.sem_inc(s_apart, 1)
                with e.Fori(0, T // 2) as it:
                    t = e.snap(it * 2)
                    t3 = e.snap(it * 2 + PAD)
                    wait(st["s_x3"], it * 2 + 2)

                    def conv(src, n):
                        for k in range(TAPS):
                            w = 2 * NI
                            last = e.tensor_tensor(prd[:, 0, w * k:w * k + w].rearrange("p (i s) -> p i s", s=2),
                                                   tap[:, k], src[:, :, bass.ds(t + k, 2)], ALU.mult)
                        last.then_inc(s, 1)
                        wait(s, it * 9 + n)
                        e.tensor_tensor(prd[:, 1, 0:64], prd[:, 0, 0:64], prd[:, 0, 64:128], ALU.add).then_inc(s, 1)
                        wait(s, it * 9 + n + 1)
                        e.tensor_tensor(prd[:, 1, 64:96], prd[:, 1, 0:32], prd[:, 1, 32:64], ALU.add).then_inc(s, 1)
                        wait(s, it * 9 + n + 2)
                    part = prd[:, 1, 64:96].rearrange("p (i s) -> p i s", s=2)
                    conv(seq, 1)
                    e.tensor_tensor(seq2[:, :, bass.ds(t3, 2)], seq[:, :, bass.ds(t3, 2)], part, ALU.add).then_inc(s, 1)
                    wait(s, it * 9 + 4)
                    conv(seq2, 5)
                    e.tensor_tensor(prd[:, 1, 96:128].rearrange("p (i s) -> p i s", s=2), part, b3x[:], ALU.add).then_inc(s, 1)
                    wait(s, it * 9 + 8)
                    e.tensor_tensor(seq[:, :, bass.ds(t, 2)], seq2[:, :, bass.ds(t3, 2)],
                                    prd[:, 1, 96:128].rearrange("p (i s) -> p i s", s=2), ALU.add).then_inc(s, 1)
                    wait(s, it * 9 + 9)

        stg = arena[:, 0:C * T].rearrange("p (c t) -> p c t", c=C)
        nat = arena[:, C * T:C * T + TB * D].rearrange("p (t n) -> p t n", t=TB)
        fv, fa, fp, fs = Queue(sem("out_dve")), Queue(sem("out_act")), Queue(sem("out_pe")), Queue([sem(f"out_dma{t}") for t in range(TB)])
        ov = out.rearrange("b (t p) n -> b p t n", p=P)
        for h in range(2):
            fv.add(f"c{h}", [(fp, "t3", True)], lambda e, b, h=h: e.tensor_copy(
                stg[:, 2 * h:2 * h + 2, :].rearrange("p (a c) t -> p a c t", a=1), seq5[:, h, bass.ds(b, 1), :, 0:T]))
        OUTB = (2, 4, 5, 6)
        for t in range(TB):
            def tr(e, b, t=t):
                for c in range(C):
                    last = e.transpose(bank[OUTB[t]][:].rearrange("p (g c j) -> p g c j", g=NG, c=C)[:, :, c, :],
                                       stg[:, c, 128 * t:128 * t + 128], ident[:])
                return last
            fp.add(f"t{t}", [(fv, "c1"), (fa, f"o{t}", True)], tr)
            fa.add(f"o{t}", [(fp, f"t{t}"), (fs, f"s{t}", True)],
                   lambda e, b, t=t: e.activation(nat[:, t, :], bank[OUTB[t]][:], ACT.Copy))
            fs.add(f"s{t}", [(fa, f"o{t}")], lambda e, b, t=t: e.dma_start(
                ov[bass.ds(b, 1), :, t, :].rearrange("a p n -> p (a n)"), nat[:, t, :]))
        with nc.Block() as block:
            @block.vector
            def _(e):
                fv.run(e, B)

            @block.tensor
            def _(e):
                fp.run(e, B)

            @block.scalar
            def _(e):
                fa.run(e, B)

            @block.sync
            def _(e):
                fs.run(e, B)
                for s in fs.sem:
                    e.wait_ge(s, (B + 1) * 16)


_INS = ['x', 'cond_2048', 'L0_cond_W_emb', 'L0_cond_b_emb', 'L0_cond_g_norm', 'L0_cond_W_qkv', 'L0_cond_g_q',
        'L0_cond_g_k', 'L0_cond_W_out', 'L1_cond_W_ih', 'L1_cond_W_hh', 'L1_cond_b_ih', 'L1_cond_b_hh', 'L3_cond_b']


def kernel(**inputs):
    import numpy as np
    import concourse.bacc as bacc
    from concourse.bass_utils import run_bass_kernel_spmd

    nc = bacc.Bacc("TRN2", target_bir_lowering=False, num_devices=1)
    arrays, args = {}, []
    for name in _INS:
        a = np.ascontiguousarray(inputs[name])
        arrays[f"in_{name}"] = a
        args.append(nc.dram_tensor(f"in_{name}", a.shape, mybir.dt.from_np(a.dtype), kind="ExternalInput").ap())
    args.append(nc.dram_tensor("out_0", (B, T, D), F32, kind="ExternalOutput").ap())
    build(nc, *args)
    r = run_bass_kernel_spmd(nc, [arrays], core_ids=[0])
    return r.results[0]["out_0"]
```

```python
import concourse.bass as bass
from concourse import mybir
from contextlib import ExitStack

F32 = mybir.dt.float32
ALU = mybir.AluOpType
ACT = mybir.ActivationFunctionType
AX = mybir.AxisListType

B, T, D, HEADS = 4, 512, 512, 16
P = 128
C = D // P
NG = 4
DH = D // HEADS
TAPS = B
PAD = TAPS - 1
TP = T + PAD
TB = T // P
NI = C * B
EPS = 1e-6


R_COND, R_GN, R_B3, R_BES, R_BEH, R_BI, R_BH, R_GQ, R_GK = 0, 4, 5, 6, 7, 8, 11, 14, 15


class Queue:

    def __init__(self, sem):
        self.sem, self.items, self.at = sem, [], {}

    def add(self, name, waits, fn):
        assert name not in self.at, name
        self.items.append((name, waits, fn))
        self.at[name] = len(self.items)

    def run(self, eng, passes, apart=None):
        dma = isinstance(self.sem, list)
        for sem in self.sem if dma else [self.sem]:
            eng.sem_inc(sem, 16 if dma else len(self.items))
        if passes == 1:
            self.one_pass(eng, 0, apart)
        else:
            with eng.Fori(0, passes) as it:
                self.one_pass(eng, it, apart)

    def one_pass(self, eng, it, apart):
        dma, passed = isinstance(self.sem, list), {}
        for i, (name, waits, fn) in enumerate(self.items):
            for w in waits:
                q, other, before = w if len(w) == 3 else (*w, False)
                if other not in q.at:
                    continue
                n, total = q.at[other], len(q.items)
                if isinstance(q.sem, list):
                    sem, value = q.sem[n - 1], (it + (1 if before else 2)) * 16
                else:
                    if before:
                        n -= total
                    if passed.get(id(q), -total) >= n:
                        continue
                    passed[id(q)] = n
                    sem, value = q.sem, it * total + (total + n)
                eng.wait_ge(sem, value)
                if apart is not None:
                    eng.sem_inc(apart, 1)
            fn(eng, it).then_inc(self.sem[i] if dma else self.sem, 16 if dma else 1)


def regroup(src, dst):
    return (src.rearrange("p (g c j) -> p c g j", g=NG, c=C), dst.rearrange("p (c g j) -> p c g j", g=NG, c=C))


def load_rows(eng, dst, src, sem):
    rows = src.rearrange("(g c j) n -> g j c n", g=NG, c=C)
    for g in range(NG):
        eng.dma_start(dst[32 * g:32 * g + 32], rows[g]).then_inc(sem, 16)


def build(nc, x, cond, W_emb, b_emb, g_norm, W_qkv, g_q, g_k, W_out, W_ih, W_hh, b_ih, b_hh, b3, out):
    with ExitStack() as ctx:
        def sb(name, shape):
            return ctx.enter_context(nc.sbuf_tensor(name, shape, F32))

        def sem(name):
            return ctx.enter_context(nc.semaphore(name))

        bank = [ctx.enter_context(nc.psum_tensor(f"bank{i}", [P, 512], F32)) for i in range(8)]

        whh = sb("whh", [P, C, 3 * D])
        seq = sb("seq", [P, NI, TP])
        ident = sb("ident", [P, P])
        vecT = sb("vecT", [P, C, 32])
        bias_g = sb("bias_g", [P, 3, C])
        tap = sb("tap", [P, TAPS, NI, 2])
        b3x = sb("b3x", [P, NI, 2])
        arena = sb("arena", [P, 48 * T])
        arena2 = sb("arena2", [P, NI * TP])
        gi = arena[:].rearrange("p (t i) -> p t i", i=48)
        seq2 = arena2[:].rearrange("p (i t) -> p i t", i=NI)
        wih = arena2[:, 0:C * 3 * D].rearrange("p (c n) -> p c n", c=C)

        at = [0]

        def take(n):
            at[0] += n
            assert at[0] <= 48 * T
            return arena[:, at[0] - n:at[0]]

        wqkv = take(C * 3 * D).rearrange("p (c n) -> p c n", c=C)
        wout = take(C * D).rearrange("p (c n) -> p c n", c=C)
        x_nat = take(TB * D).rearrange("p (t n) -> p t n", t=TB)
        xp = take(TB * D).rearrange("p (t n) -> p t n", t=TB)
        xnT = take(C * T).rearrange("p (c t) -> p c t", c=C)
        v_nat = take(TB * D).rearrange("p (t n) -> p t n", t=TB)
        oT = take(C * T).rearrange("p (c t) -> p c t", c=C)
        kT = take(2 * T).rearrange("p (a t) -> p a t", a=2)
        qm = take(2 * NG * T).rearrange("p (a g t) -> p a g t", a=2, g=NG)
        qn = take(T)
        sqb = take(T)
        wemb = arena2[:, 0:C * 2 * D].rearrange("p (c n) -> p c n", c=C)
        stage = oT[:, 0, 0:P]
        rnb = sb("rnb", [P, T])
        pT = arena2[:, 0:NG * TB * T].rearrange("p (g b n) -> p g b n", g=NG, b=TB)
        NP = 8
        prob = sb("prob", [P, NP, T])
        small = sb("small", [P, 64])
        mn, sm, ri = small[:, 0:8], small[:, 8:16], small[:, 16:24]
        ssx, lnx, rsx = small[:, 24:28], small[:, 28:32], small[:, 32:36]
        cur = small[:, 36:44].rearrange("p (s c) -> p s c", s=2)
        eps = small[:, 44:45]
        maskn = small[:, 45:49]
        modT = sb("modT", [P, 2, C, B])
        ones = sb("ones", [P, P])

        s_const = sem("s_const")
        s_id = sem("s_id")
        s_wl = sem("s_wl")
        s_vec = sem("s_vec")
        s_emb = sem("s_emb")
        s_mod = sem("s_mod")
        s_modT = sem("s_modT")
        s_wkv = sem("s_wkv")
        s_wout = sem("s_wout")
        n_vec = 4 * 11 + 2 * NG
        with nc.Block() as block:
            @block.sync
            def _(e):
                e.wait_ge(s_const, 1)
                for g in range(NG):
                    cols = slice(128 * g, 128 * g + 128)
                    e.dma_start(stage[32 * g:32 * g + B, :], cond[:, cols]).then_inc(s_vec, 16)
                    rows = [(R_GN, g_norm[cols]), (R_B3, b3[cols]), (R_BES, b_emb[cols]),
                            (R_BEH, b_emb[D + 128 * g:D + 128 * g + 128])]
                    rows += [(R_BI + q, b_ih[q * D + 128 * g:q * D + 128 * g + 128]) for q in range(3)]
                    rows += [(R_BH + q, b_hh[q * D + 128 * g:q * D + 128 * g + 128]) for q in range(3)]
                    for r, v in rows:
                        e.dma_start(stage[32 * g + r:32 * g + r + 1, :],
                                    v.rearrange("(a n) -> a n", a=1)).then_inc(s_vec, 16)
                    for r, v in ((R_GQ, g_q), (R_GK, g_k)):
                        e.dma_start(stage[32 * g + r:32 * g + r + 1, 0:DH],
                                    v.rearrange("(a n) -> a n", a=1)).then_inc(s_vec, 16)

            @block.scalar
            def _(e):
                load_rows(e, wemb, W_emb, s_emb)
                load_rows(e, whh[:], W_qkv, s_wkv)
                load_rows(e, x_nat, W_out, s_wout)
                e.wait_ge(s_wkv, NG * 16)
                for i in range(3 * C):
                    if i % 2 == 0:
                        a, b = regroup(whh[:, i // 3, i % 3 * D:i % 3 * D + D], wqkv[:, i // 3, i % 3 * D:i % 3 * D + D])
                        e.activation(b, a, ACT.Copy)

            @block.gpsimd
            def _(e):
                e.memset(ident[:], 0.0).then_inc(s_id, 1)
                e.wait_ge(s_id, 1)
                e.affine_select(out=ident[:], in_=ident[:], compare_op=ALU.not_equal, fill=1.0, base=0,
                                pattern=[[-1, P]], channel_multiplier=1).then_inc(s_id, 1)
                e.memset(seq[:, :, 0:PAD], 0.0).then_inc(s_id, 1)

            @block.vector
            def _(e):
                e.memset(stage, 0.0).then_inc(s_const, 1)
                e.memset(bank[0][:], 0.0).then_inc(s_const, 1)
                e.memset(ones[:], 0.0).then_inc(s_const, 1)
                e.memset(maskn, 0.0).then_inc(s_const, 1)
                e.memset(eps, EPS).then_inc(s_const, 1)
                e.wait_ge(s_const, 5)
                for g in range(NG):
                    q = slice(32 * g, 32 * g + 32)
                    e.memset(ones[q, q], 1.0).then_inc(s_const, 1)
                    e.memset(maskn[q, g:g + 1], -float(DH) ** -0.5).then_inc(s_const, 1)
                e.wait_ge(s_vec, n_vec * 16)
                e.transpose(vecT[:], stage.rearrange("p (c i) -> p c i", c=C)).then_inc(s_mod, 1)
                e.wait_ge(s_mod, 1)
                for q in range(2):
                    e.tensor_tensor(bias_g[:, q, :], vecT[:, :, R_BI + q], vecT[:, :, R_BH + q],
                                    ALU.add).then_inc(s_mod, 1)
                e.tensor_copy(bias_g[:, 2, :], vecT[:, :, R_BI + 2]).then_inc(s_mod, 1)
                for h in range(2):
                    for b in range(B):
                        for s in range(2):
                            i = (h * B + b) * 2
                            e.tensor_copy(tap[:, :, i:i + 2, s],
                                          vecT[:, 2 * h:2 * h + 2, 0:TAPS].rearrange("p c k -> p k c"))
                            e.tensor_copy(b3x[:, i:i + 2, s], vecT[:, 2 * h:2 * h + 2, R_B3]).then_inc(s_mod, 1)
                e.wait_ge(s_wkv, NG * 16)
                for i in range(3 * C):
                    if i % 2:
                        a, b = regroup(whh[:, i // 3, i % 3 * D:i % 3 * D + D], wqkv[:, i // 3, i % 3 * D:i % 3 * D + D])
                        e.tensor_copy(b, a)
                e.wait_ge(s_wout, NG * 16)
                for k in range(C):
                    a, b = regroup(x_nat[:, k, :], wout[:, k, :])
                    e.tensor_copy(b, a)
                e.wait_ge(s_modT, 1)
                sT = xp[:, 0, 0:256].rearrange("p (q c i) -> p q c i", q=2, c=C)
                e.transpose(sT, bank[0][:, 0:256].rearrange("p (q c i) -> p q c i", q=2, c=C)).then_inc(s_modT, 1)
                e.wait_ge(s_modT, 2)
                for c in range(C):
                    e.tensor_scalar(modT[:, 0, c, :], sT[:, 0, c, 0:B], vecT[:, c, R_BES:R_BES + 1], 1.0,
                                    ALU.add, ALU.add).then_inc(s_modT, 1)
                    e.tensor_scalar(modT[:, 1, c, :], sT[:, 1, c, 0:B], vecT[:, c, R_BEH:R_BEH + 1], None,
                                    ALU.add).then_inc(s_modT, 1)
                e.wait_ge(s_modT, 2 + 2 * C)
                for c in range(C):
                    e.tensor_scalar(modT[:, 0, c, :], modT[:, 0, c, :], vecT[:, c, R_GN:R_GN + 1], None,
                                    ALU.mult).then_inc(s_modT, 1)

            @block.tensor
            def _(e):
                e.wait_ge(s_emb, NG * 16)
                e.wait_ge(s_const, 2)
                e.wait_ge(s_mod, 1)
                wv = wemb.rearrange("p c (q G n) -> p c q G n", q=2, G=NG)
                for k in range(C):
                    for G in range(NG):
                        last = e.matmul(bank[0][32 * G:32 * G + B, 0:256], vecT[:, k, 0:B], wv[:, k, :, G, :],
                                        start=k == 0, stop=k == C - 1)
                last.then_inc(s_modT, 1)

        xv = x.rearrange("b (t p) n -> b p t n", p=P)
        seq5 = seq[:].rearrange("p (h b c) t -> p h b c t", h=2, b=B)

        def seq_at(c, b):
            return seq5[:, c // 2, bass.ds(b, 1), c % 2, PAD:TP]

        NS, QK, SS, OB = 3, 5, 6, 7
        OBANK = [5, 6, 7, 4]
        LAG = 3
        NM = HEADS * TB
        MC = NG * TB
        wq = wqkv.rearrange("p k (s c n) -> p k s c n", s=3, c=C)
        wo = wout.rearrange("p k (c n) -> p k c n", c=C)

        def phase(name, batches, attend, prepare):
            qs_, qa, qv, qg, qp = (Queue([sem(name + "_load")]), Queue(sem(name + "_act")), Queue(sem(name + "_dve")),
                                   Queue(sem(name + "_pool")), Queue(sem(name + "_pe")))
            first = batches[0]

            def following(b):
                return b + (first + 1)

            def own(b):
                return b + first

            def load_x():
                qs_.add("x", [(qa, "sq3", True), (qa, "xp3", True)],
                        lambda e, b: e.dma_start(x_nat, xv[bass.ds(following(b), 1)].rearrange("a p t n -> p (a t) n")))
                qv.add("cur", [], lambda e, b: e.tensor_copy(
                    cur, modT[:].rearrange("p s c b -> p (s c) b")[:, :, bass.ds(following(b), 1)]
                    .rearrange("p (s c) b -> p s (c b)", s=2)))

            def squares(t):
                qa.add(f"sq{t}", [(qs_, "x"), (qp, "ks3")] + [(qa, f"sq{t - 1}")] * (t > 0),
                       lambda e, b: e.activation(sqb, x_nat[:, t, :], ACT.Square, accum_out=ssx[:, t:t + 1]))
                if t == TB - 1:
                    qa.add("lnx", [(qa, "sq3")], lambda e, b: e.activation(lnx, ssx, ACT.Ln, bias=eps, scale=1.0 / D))
                    qa.add("rsx", [(qa, "lnx")], lambda e, b: e.activation(rsx, lnx, ACT.Exp, scale=-0.5))

            def group(t):
                def copy(e, b):
                    src, dst = regroup(x_nat[:, t, :], xp[:, t, :])
                    return e.activation(dst, src, ACT.Copy)
                qa.add(f"xp{t}", [(qs_, "x"), (qg, "o23", True)], copy)

            def transposes(e, dst, c):
                for t in range(TB):
                    last = e.transpose(dst[:, 128 * t:128 * t + 128], xp[:, t, 128 * c:128 * c + 128], ident[:])
                return last

            def turn_x(c):
                prior = (qa, f"xr{c - 2}") if c >= 2 else ((qv, "kn3"), (qa, "kl3"))[c]
                qp.add(f"tx{c}", [(qa, "xp3"), prior], lambda e, b: transposes(e, bank[5 + c % 2], c))
                qa.add(f"xr{c}", [(qp, f"tx{c}")],
                       lambda e, b: e.activation(seq_at(c, following(b)),
                                                 bank[5 + c % 2][:].rearrange("p (a t) -> p a t", a=1), ACT.Copy))

            def scale_x(t):
                qv.add(f"xn{t}", [(qa, "rsx"), (qp, "tx3")],
                       lambda e, b: e.tensor_scalar(xp[:, t, :], xp[:, t, :], rsx[:, t:t + 1], None, ALU.mult))

            def turn_xn(c):
                qp.add(f"tn{c}", [(qv, "xn3"), (qv, f"xt{c - 2}") if c >= 2 else (qa, f"xr{c + 2}")],
                       lambda e, b: transposes(e, bank[5 + c % 2], c))
                qv.add(f"xt{c}", [(qp, f"tn{c}"), (qp, "k3"), (qv, "cur")],
                       lambda e, b: e.tensor_scalar(xnT[:, c, :], bank[5 + c % 2][:], cur[:, 0, c:c + 1],
                                                    cur[:, 1, c:c + 1], ALU.mult, ALU.add))

            def project_v(t):
                def vproj(e, b):
                    for k in range(C):
                        last = e.matmul(bank[OB][:], xnT[:, k, 128 * t:128 * t + 128], wqkv[:, k, 2 * D:3 * D],
                                        start=k == 0, stop=k == C - 1)
                    return last
                qp.add(f"v{t}", [(qa, f"ve{t - 1}") if t else (qv, "o12", True)], vproj)
                qa.add(f"ve{t}", [(qp, f"v{t}"), (qp, "pv3", True)],
                       lambda e, b: e.activation(v_nat[:, t, :], bank[OB][:], ACT.Copy))

            def tiles_done(c):
                return (qp, f"S{MC * (c - 2) + MC - 1}") if c >= 2 else (
                    (qp, f"S{NM - 1}", True) if c else (qp, f"S{3 * MC - 1}"))

            def norm_start(s, c):
                n = "qk"[s]
                prior = (qv, f"qn{c}") if s else ((qv, "xt3"), (qv, "o10", True), (qv, "kn1"), (qv, "kn2"))[c]

                def proj(e, b):
                    for k in range(C):
                        last = e.matmul(bank[QK][:], wq[:, k, s, c], xnT[:, k, :], start=k == 0, stop=k == C - 1)
                    return last
                read = (qp, f"qs{c}") if s else ((qa, "sq3"), (qp, "ks0", True), (qp, "ks1"), (qp, "ks2"))[c]
                qp.add(f"{n}{c}", [prior], proj)
                qa.add(f"{n}2{c}", [(qp, f"{n}{c}"), read],
                       lambda e, b: e.activation(sqb, bank[QK][:], ACT.Square))

            def norm_end(s, c):
                n = "qk"[s]
                prior = (qa, f"ql{c}") if s else ((qv, "xt3"), (qv, "o11", True), (qa, "kl1"), (qa, "kl2"))[c]
                qp.add(f"{n}s{c}", [(qa, f"{n}2{c}"), prior],
                       lambda e, b: e.matmul(bank[SS][:], ones[:], sqb, start=True, stop=True))
                used = (qv, f"qn{c}") if s else ((qv, "kn3"), (qv, "kn0", True), (qv, "kn1"), (qv, "kn2"))[c]
                qa.add(f"{n}l{c}", [(qp, f"{n}s{c}"), used],
                       lambda e, b: e.activation(rnb[:], bank[SS][:], ACT.Ln, bias=eps, scale=1.0 / DH))
                qa.add(f"{n}r{c}", [(qa, f"{n}l{c}")],
                       lambda e, b: e.activation(rnb[:], rnb[:], ACT.Exp, scale=-0.5))
                if s == 0:
                    masked = ((qg, "qm33"), (qg, "qm03", True), (qg, "qm13"), (qg, "qm23"))[c]
                    qv.add(f"qn{c}", [(qa, f"qr{c}"), masked],
                           lambda e, b: e.scalar_tensor_tensor(qn, bank[QK][:], vecT[:, 0, R_GQ:R_GQ + 1], rnb[:],
                                                               ALU.mult, ALU.mult))
                    for g in range(NG):
                        qg.add(f"qm{c}{g}", [(qv, f"qn{c}"), tiles_done(c)],
                               lambda e, b, g=g: e.tensor_scalar(qm[:, c % 2, g, :], qn, maskn[:, g:g + 1], 1.0,
                                                                 ALU.mult, ALU.mult))
                else:
                    qv.add(f"kn{c}", [(qa, f"kr{c}"), tiles_done(c)],
                           lambda e, b: e.scalar_tensor_tensor(kT[:, c % 2, :], bank[QK][:], vecT[:, 0, R_GK:R_GK + 1],
                                                               rnb[:], ALU.mult, ALU.mult))

            def before(q, name, m, n):
                return (q, f"{name}{m - n}") if m >= n else (q, f"{name}{NM + m - n}", True)

            def slot(m):
                return slice(m % NP, m % NP + 1)

            def products(m):
                c, g, t = m // MC, m // TB % NG, m % TB
                free = (qa, f"e{m - NS}") if m >= NS else (qa, f"e{NM - 1}", True)
                qp.add(f"S{m}", [(qg, f"qm{c}3", c == 0), (qv, f"kn{c}", c == 0), free],
                       lambda e, b: e.matmul(bank[m % NS][:], qm[:, c % 2, g, 128 * t:128 * t + 128], kT[:, c % 2, :],
                                             start=True, stop=True))
                qv.add(f"mn{m}", [(qp, f"S{m}"), before(qa, "e", m, NP)],
                       lambda e, b: e.tensor_reduce(mn[:, slot(m)], bank[m % NS][:], AX.X, ALU.min))

            def exponentials(m):
                qa.add(f"e{m}", [(qv, f"mn{m}"), before(qp, "T", m, NP), before(qv, "ri", m, NP)],
                       lambda e, b: e.activation(prob[:, m % NP, :], bank[m % NS][:], ACT.Exp, bias=mn[:, slot(m)],
                                                 scale=-1.0, accum_out=sm[:, slot(m)]))

            def normalise(m):
                qv.add(f"ri{m}", [(qa, f"e{m}"), before(qg, "n", m, NP)],
                       lambda e, b: e.reciprocal(ri[:, slot(m)], sm[:, slot(m)]))
                qg.add(f"n{m}", [(qv, f"ri{m}")],
                       lambda e, b: e.tensor_scalar(prob[:, m % NP, :], prob[:, m % NP, :], ri[:, slot(m)], 1.0,
                                                    ALU.mult, ALU.mult))

            def turn(m):
                g, t = m // TB % NG, m % TB
                dst = bank[3 + m % 2]

                def tr(e, b):
                    for k in range(TB):
                        last = e.transpose(dst[:, 128 * k:128 * k + 128], prob[:, m % NP, 128 * k:128 * k + 128],
                                           ident[:])
                    return last
                qe = (qa, qv)[m % 2]
                prior = (qe, f"p{m - 2}") if m >= 2 else ((qv, "o13", True) if m else (qa, f"p{NM - 2}", True))
                qp.add(f"T{m}", [(qg, f"n{m}"), prior], tr)
                free = (qp, f"pv{m // MC - 1}") if m >= MC else (qp, "pv3", True)
                if m % 2 == 0:
                    qa.add(f"p{m}", [(qp, f"T{m}"), free], lambda e, b: e.activation(pT[:, g, t, :], dst[:], ACT.Copy))
                else:
                    qv.add(f"p{m}", [(qp, f"T{m}"), free], lambda e, b: e.tensor_copy(pT[:, g, t, :], dst[:]))

            def values(c):
                def pv(e, b):
                    for k in range(TB):
                        for g in range(NG):
                            last = e.matmul(bank[OB][32 * g:32 * g + DH, :],
                                            v_nat[:, k, 128 * c + 32 * g:128 * c + 32 * g + DH],
                                            pT[:, g, :, 128 * k:128 * k + 128], start=k == 0, stop=k == TB - 1)
                    return last
                qp.add(f"pv{c}", [(qa, f"p{MC * c + MC - 2}"), (qv, f"p{MC * c + MC - 1}"), (qa, "ve3"),
                                  (qa, f"oe{c - 1}" if c else "ve3")], pv)
                qa.add(f"oe{c}", [(qp, f"pv{c}"), (qv, "o13", True)],
                       lambda e, b: e.activation(oT[:, c, :], bank[OB][:], ACT.Copy))

            def project_o(c):
                def oproj(e, b):
                    for k in range(C):
                        last = e.matmul(bank[OBANK[c]][:], wo[:, k, c], oT[:, k, :], start=k == 0, stop=k == C - 1)
                    return last
                prior = [[(qv, "kn0"), (qv, "kn3")], [(qa, "kl0"), (qa, "kl3")], [], [(qv, f"p{NM - 1}")]][c]
                qp.add(f"op{c}", [(qa, "oe3")] + prior, oproj)
                tmp = xp[:, c, :]
                qv.add(f"o1{c}", [(qp, f"op{c}"), (qg, f"o2{c}", True)],
                       lambda e, b: e.tensor_tensor(tmp, bank[OBANK[c]][:], oT[:, c, :], ALU.add))
                qg.add(f"o2{c}", [(qv, f"o1{c}"), (qa, f"xr{c}", True)],
                       lambda e, b: e.tensor_tensor(seq_at(c, own(b)), seq_at(c, own(b)),
                                                    tmp.rearrange("p (a t) -> p a t", a=1), ALU.add))

            if prepare:
                load_x()
            beside = {m: [] for m in range(NM + LAG + 1)}
            if attend:
                for c in range(1, C):
                    m = MC * (c - 1)
                    for off, f, s in ((1, norm_start, 0), (4, norm_end, 0), (7, norm_start, 1), (10, norm_end, 1)):
                        beside[m + off].append((f, s, c))
                for t in range(TB):
                    beside[2 + 4 * t].append((project_v, t))
            if prepare:
                for t in range(TB):
                    beside[40 + t].append((group, t))
                    beside[44 + t].append((squares, t))
                    beside[45 + t].append((turn_x, t))
                    beside[49 + t // 2].append((scale_x, t))
                    beside[52 + t].append((turn_xn, t))
                for m, f, s in ((56, norm_start, 0), (58, norm_end, 0), (60, norm_start, 1), (62, norm_end, 1)):
                    beside[m].append((f, s, 0))
            for m in range(NM + LAG + 1):
                if attend:
                    if m < NM:
                        products(m)
                    if m > LAG and m % MC == LAG:
                        values(m // MC - 1)
                    if LAG <= m < NM + LAG:
                        turn(m - LAG)
                    if m < NM:
                        exponentials(m)
                    if 1 <= m <= NM:
                        normalise(m - 1)
                for f, *args in beside[m]:
                    f(*args)
            if attend:
                for c in range(C):
                    project_o(c)

            passes = len(batches)
            with nc.Block() as block:
                @block.sync
                def _(e):
                    if attend and prepare:
                        load_rows(e, whh[:], W_hh, s_whh)
                    if prepare:
                        qs_.run(e, passes)
                    else:
                        e.wait_ge(qp.sem, len(qp.items) * passes + qp.at["k3"])
                        load_rows(e, wqkv, W_ih, s_wih)
                        e.wait_ge(s_whh, NG * 16)
                        e.wait_ge(s_wih, NG * 16)

                @block.scalar
                def _(e):
                    e.preload_act_table_set("natural_log_exp_and_others")
                    qa.run(e, passes)

                @block.vector
                def _(e):
                    qv.run(e, passes)

                @block.gpsimd
                def _(e):
                    qg.run(e, passes, apart=s_apart)

                @block.tensor
                def _(e):
                    qp.run(e, passes)

        s_wih = sem("s_wih")
        s_whh = sem("s_whh")
        s_reg = sem("s_reg")
        s_apart = sem("s_apart")
        phase("first", [-1], attend=False, prepare=True)
        phase("most", list(range(B - 1)), attend=True, prepare=True)
        phase("last", [B - 1], attend=True, prepare=False)

        ga, gv, gp = Queue(sem("gi_act")), Queue(sem("gi_dve")), Queue(sem("gi_pe"))
        wi = wih.rearrange("p k (q c n) -> p k q c n", q=3, c=C)
        gi6 = arena[:].rearrange("p (t q h b c) -> p t q h b c", q=3, h=2, b=B, c=2)
        for i in range(3 * C):
            q, c = i // C, i % C

            def prod(e, b, i=i, q=q, c=c):
                for k in range(C):
                    last = e.matmul(bank[i % 6][:], wi[:, k, q, c], seq_at(k, b), start=k == 0, stop=k == C - 1)
                return last
            qe = (ga, gv)[i % 2]
            gp.add(f"g{i}", [(qe, f"g{i - 6}") if i >= 6 else (qe, f"g{i + 6}", True)], prod)
            dst = gi6[:, :, q, c // 2, :, c % 2]
            if i % 2 == 0:
                ga.add(f"g{i}", [(gp, f"g{i}")], lambda e, b, i=i, q=q, c=c, dst=dst: e.activation(
                    dst[:, :, bass.ds(b, 1)], bank[i % 6][:].rearrange("p (t a) -> p t a", a=1), ACT.Identity,
                    bias=bias_g[:, q, c:c + 1]))
            else:
                gv.add(f"g{i}", [(gp, f"g{i}")], lambda e, b, i=i, q=q, c=c, dst=dst: e.tensor_scalar(
                    dst[:, :, bass.ds(b, 1)], bank[i % 6][:].rearrange("p (t a) -> p t a", a=1),
                    bias_g[:, q, c:c + 1], None, ALU.add))
        with nc.Block() as block:
            def regroup_ih(e, first, copy):
                for i in range(first, 3 * C, 2):
                    a, b = regroup(wqkv[:, i // 3, i % 3 * D:i % 3 * D + D], wih[:, i // 3, i % 3 * D:i % 3 * D + D])
                    copy(b, a).then_inc(s_reg, 1)
                e.wait_ge(s_reg, 3 * C)

            @block.tensor
            def _(e):
                e.wait_ge(s_reg, 3 * C)
                gp.run(e, B)

            @block.scalar
            def _(e):
                regroup_ih(e, 0, lambda b, a: e.activation(b, a, ACT.Copy))
                ga.run(e, B)

            @block.vector
            def _(e):
                regroup_ih(e, 1, lambda b, a: e.tensor_copy(b, a))
                gv.run(e, B)

        used = [0]
        prob_flat = prob[:].rearrange("p a t -> p (a t)")

        def tile(shape):
            n = 1
            for d in shape[1:]:
                n *= d
            used[0] += n
            assert used[0] <= NP * T
            v = prob_flat[:, used[0] - n:used[0]]
            return v if len(shape) == 2 else v.rearrange("p (a b) -> p a b", a=shape[1])

        hb = tile([P, 2, 4 * NI])
        tr_rz = tile([P, 2, P])
        s_rz_ = tile([P, 2 * NI])
        gin = tile([P, 2, 2 * NI])
        r_d0 = tile([P, 2 * NI])
        n_d1 = tile([P, 2, P])
        scA = tile([P, 2 * NI])
        m_d0 = tile([P, 4 * NI])
        z_d1 = tile([P, 4 * NI])
        brow = tile([P, NG, P])
        row0 = tile([P, B])
        prd = tile([P, 2, TAPS * NI * 2])
        st = {n: sem(n) for n in ("s_clear", "s_brow", "s_h", "s_rz", "s_n", "s_tr", "s_sum", "s_sig", "s_pre", "s_gi",
                                  "s_tanh", "s_hold", "s_x3", "s_pool")}
        RZ, BN = 0, ((1, 2), (3, 4))

        def every(ap, n):
            return ap.rearrange("p (i s) -> p i s", s=n)

        N_CLEAR = 14
        with nc.Block() as block:
            @block.sync
            def _(e):
                e.wait_ge(st["s_clear"], 1)
                e.dma_start(brow[0:1], b_hh[2 * D:3 * D].rearrange("(a g n) -> a g n", a=1, g=NG)).then_inc(st["s_brow"], 16)
                e.wait_ge(st["s_brow"], 16)

            @block.vector
            def _(e):
                c = st["s_clear"]
                e.memset(brow[:], 0.0).then_inc(c, 1)
                for v in (row0[:], r_d0[:], m_d0[:], n_d1[:], bank[RZ][:], bank[1][:], bank[2][:], bank[3][:],
                          bank[4][:], seq2[:, :, 0:PAD]):
                    e.memset(v, 0.0).then_inc(c, 1)
                e.memset(z_d1[:], -1.0).then_inc(c, 1)
                e.wait_ge(c, 12)
                e.memset(row0[0:1, :], 1.0).then_inc(c, 1)
                e.memset(every(z_d1[:], 4)[:, :, 0], 0.0).then_inc(c, 1)
                e.wait_ge(c, N_CLEAR)
                with e.Fori(0, T // 2) as it:
                    for u in range(2):
                        t = it * 2 + u
                        t1, h1, h2 = e.snap(t + 1), e.snap(2 * t + 1), e.snap(2 * t + 2)
                        t4 = [e.snap(4 * t + i) for i in (1, 2, 3, 4)]
                        h4 = e.snap(2 * t + 4)
                        now = e.snap(t + PAD)

                        def turn_rz(q):
                            e.transpose(tr_rz[:, q, :].rearrange("p (h i c) -> p h c i", c=2, h=2),
                                        bank[RZ][:, P * q:P * q + P].rearrange("p (h c i) -> p h c i", h=2, c=2)
                                        ).then_inc(st["s_tr"], 1)

                        def add_gi(q):
                            s = slice(NI * q, NI * q + NI)
                            e.tensor_tensor(s_rz_[:, s].rearrange("p (h i) -> p h i", h=2),
                                            tr_rz[:, q, :].rearrange("p (h i) -> p h i", h=2)[:, :, 0:8],
                                            gin[:, u, s].rearrange("p (h i) -> p h i", h=2),
                                            ALU.add).then_inc(st["s_sum"], 1)

                        def turn_n(h):
                            e.wait_ge(st["s_n"], (h1, h2)[h])
                            e.transpose(n_d1[:, h, :].rearrange("p (i c s) -> p c i s", c=2, s=2)[:, :, :, 0],
                                        bank[BN[h][u]][:, 0:64].rearrange("p (c i) -> p c i", c=2)
                                        ).then_inc(st["s_tr"], 1)

                        def scan_a(h):
                            s = slice(NI * h, NI * h + NI)
                            e.tensor_tensor_scan(scA[:, s], r_d0[:, s], n_d1[:, h, 0:NI], 0.0, ALU.mult, ALU.add
                                                 ).then_inc(st["s_pre"], 1)

                        def scan_b(h):
                            e.wait_ge(st["s_tanh"], (h1, h2)[h])
                            s = slice(2 * NI * h, 2 * NI * h + 2 * NI)
                            e.tensor_tensor_scan(hb[:, 1 - u, s], m_d0[:, s], z_d1[:, s], 0.0, ALU.subtract, ALU.mult
                                                 ).then_inc(st["s_h"], 1)

                        e.wait_ge(st["s_gi"], t1)
                        e.wait_ge(st["s_rz"], t1)
                        turn_rz(0)
                        e.wait_ge(st["s_tr"], t4[0])
                        add_gi(0)
                        turn_rz(1)
                        turn_n(0)
                        e.wait_ge(st["s_tr"], t4[1])
                        add_gi(1)
                        e.wait_ge(st["s_tr"], t4[2])
                        e.wait_ge(st["s_sig"], h1)
                        scan_a(0)
                        scan_b(0)
                        turn_n(1)
                        e.wait_ge(st["s_tr"], t4[3])
                        scan_a(1)
                        scan_b(1)
                        e.wait_ge(st["s_h"], h4)
                        e.tensor_tensor(seq[:, :, bass.ds(now, 1)], seq[:, :, bass.ds(now, 1)],
                                        every(hb[:, 1 - u, :], 4)[:, :, 3:4], ALU.add).then_inc(st["s_x3"], 1)

            @block.scalar
            def _(e):
                e.wait_ge(st["s_clear"], N_CLEAR)
                e.preload_act_table_set("sigmoid_and_others")
                n_in = n_d1[:, :, 0:NI].rearrange("p h (i s) -> p h i s", s=2)[:, :, :, 1]

                def bring(t, u):
                    e.activation(gin[:, u:u + 1, :], gi[:, bass.ds(t, 1), 0:2 * NI], ACT.Copy)
                    e.activation(n_in, gi[:, bass.ds(t, 1), 2 * NI:3 * NI].rearrange("p a (h i) -> p (a h) i", h=2),
                                 ACT.Copy).then_inc(st["s_gi"], 1)
                for h in range(2):
                    src = vecT[:, 2 * h:2 * h + 2, 0:B].rearrange("p c b -> p b c")
                    s = slice(2 * NI * h, 2 * NI * h + 2 * NI)
                    e.activation(hb[:, 0, s].rearrange("p (b c s) -> p b c s", b=B, c=2)[:, :, :, 3], src, ACT.Copy)
                    e.activation(m_d0[:, s].rearrange("p (b c s) -> p b c s", b=B, c=2)[:, :, :, 2], src,
                                 ACT.Copy).then_inc(st["s_h"], 1)
                with e.Fori(0, T // 2) as it:
                    for u in range(2):
                        t = it * 2 + u
                        h1, h2, h4 = e.snap(2 * t + 1), e.snap(2 * t + 2), e.snap(2 * t + 4)
                        bring(e.snap(t), u)
                        e.wait_ge(st["s_sum"], h1)
                        e.activation(every(r_d0[:], 2)[:, :, 1], s_rz_[:, 0:NI], ACT.Sigmoid).then_inc(st["s_sig"], 1)
                        e.wait_ge(st["s_sum"], h2)
                        e.activation(every(z_d1[:], 4)[:, :, 2], s_rz_[:, NI:2 * NI], ACT.Sigmoid).then_inc(st["s_sig"], 1)
                        for h in range(2):
                            e.wait_ge(st["s_pre"], (h1, h2)[h])
                            pre = every(scA[:, NI * h:NI * h + NI], 2)[:, :, 1:2]
                            dst = m_d0[:, 2 * NI * h:2 * NI * h + 2 * NI].rearrange("p (i a s) -> p i a s", a=2, s=2)
                            e.activation(dst[:, :, :, 1], pre.broadcast_to([P, 8, 2]), ACT.Tanh, scale=-1.0
                                         ).then_inc(st["s_tanh"], 1)
                        e.wait_ge(st["s_h"], h4)
                        e.activation(every(m_d0[:], 4)[:, :, 2], every(hb[:, 1 - u, :], 4)[:, :, 3], ACT.Copy)

            @block.tensor
            def _(e):
                e.wait_ge(st["s_clear"], N_CLEAR)
                e.wait_ge(st["s_brow"], 16)

                def bias(u):
                    for h in range(2):
                        for G in range(NG):
                            e.matmul(bank[BN[h][u]][32 * G:32 * G + B, 0:64], row0[:], brow[:, G, 64 * h:64 * h + 64],
                                     start=True, stop=False)
                bias(0)
                wv = whh[:].rearrange("p c (q G n) -> p c q G n", q=3, G=NG)
                with e.Fori(0, T // 2) as it:
                    for u in range(2):
                        t = it * 2 + u
                        h1, h2 = e.snap(2 * t + 1), e.snap(2 * t + 2)
                        hv = hb[:, u, :].rearrange("p (h b c s) -> p h b c s", h=2, c=2, s=4)
                        for k in range(C):
                            if k % 2 == 0:
                                e.wait_ge(st["s_h"], (h1, h2)[k // 2])
                            for G in range(NG):
                                last = e.matmul(bank[RZ][32 * G:32 * G + B, 0:2 * P], hv[:, k // 2, :, k % 2, 3],
                                                wv[:, k, 0:2, G, :], start=k == 0, stop=k == C - 1)
                        last.then_inc(st["s_rz"], 1)
                        for h in range(2):
                            for k in range(C):
                                for G in range(NG):
                                    last = e.matmul(bank[BN[h][u]][32 * G:32 * G + B, 0:64],
                                                    hv[:, k // 2, :, k % 2, 3],
                                                    wv[:, k, 2, G, 64 * h:64 * h + 64], start=False, stop=k == C - 1)
                            last.then_inc(st["s_n"], 1)
                        bias(1 - u)

            @block.gpsimd
            def _(e):
                e.wait_ge(st["s_clear"], N_CLEAR)
                s = st["s_pool"]

                def wait(sem_, n):
                    e.wait_ge(sem_, n)
                    e.sem_inc(s_apart, 1)
                with e.Fori(0, T // 2) as it:
                    t = e.snap(it * 2)
                    t3 = e.snap(it * 2 + PAD)
                    wait(st["s_x3"], it * 2 + 2)

                    def conv(src, n):
                        for k in range(TAPS):
                            w = 2 * NI
                            last = e.tensor_tensor(prd[:, 0, w * k:w * k + w].rearrange("p (i s) -> p i s", s=2),
                                                   tap[:, k], src[:, :, bass.ds(t + k, 2)], ALU.mult)
                        last.then_inc(s, 1)
                        wait(s, it * 9 + n)
                        e.tensor_tensor(prd[:, 1, 0:64], prd[:, 0, 0:64], prd[:, 0, 64:128], ALU.add).then_inc(s, 1)
                        wait(s, it * 9 + n + 1)
                        e.tensor_tensor(prd[:, 1, 64:96], prd[:, 1, 0:32], prd[:, 1, 32:64], ALU.add).then_inc(s, 1)
                        wait(s, it * 9 + n + 2)
                    part = prd[:, 1, 64:96].rearrange("p (i s) -> p i s", s=2)
                    conv(seq, 1)
                    e.tensor_tensor(seq2[:, :, bass.ds(t3, 2)], seq[:, :, bass.ds(t3, 2)], part, ALU.add).then_inc(s, 1)
                    wait(s, it * 9 + 4)
                    conv(seq2, 5)
                    e.tensor_tensor(prd[:, 1, 96:128].rearrange("p (i s) -> p i s", s=2), part, b3x[:], ALU.add).then_inc(s, 1)
                    wait(s, it * 9 + 8)
                    e.tensor_tensor(seq[:, :, bass.ds(t, 2)], seq2[:, :, bass.ds(t3, 2)],
                                    prd[:, 1, 96:128].rearrange("p (i s) -> p i s", s=2), ALU.add).then_inc(s, 1)
                    wait(s, it * 9 + 9)

        stg = arena[:, 0:C * T].rearrange("p (c t) -> p c t", c=C)
        nat = arena[:, C * T:C * T + TB * D].rearrange("p (t n) -> p t n", t=TB)
        fv, fa, fp, fs = Queue(sem("out_dve")), Queue(sem("out_act")), Queue(sem("out_pe")), Queue([sem(f"out_dma{t}") for t in range(TB)])
        ov = out.rearrange("b (t p) n -> b p t n", p=P)
        for h in range(2):
            fv.add(f"c{h}", [(fp, "t3", True)], lambda e, b, h=h: e.tensor_copy(
                stg[:, 2 * h:2 * h + 2, :].rearrange("p (a c) t -> p a c t", a=1), seq5[:, h, bass.ds(b, 1), :, 0:T]))
        OUTB = (2, 4, 5, 6)
        for t in range(TB):
            def tr(e, b, t=t):
                for c in range(C):
                    last = e.transpose(bank[OUTB[t]][:].rearrange("p (g c j) -> p g c j", g=NG, c=C)[:, :, c, :],
                                       stg[:, c, 128 * t:128 * t + 128], ident[:])
                return last
            fp.add(f"t{t}", [(fv, "c1"), (fa, f"o{t}", True)], tr)
            fa.add(f"o{t}", [(fp, f"t{t}"), (fs, f"s{t}", True)],
                   lambda e, b, t=t: e.activation(nat[:, t, :], bank[OUTB[t]][:], ACT.Copy))
            fs.add(f"s{t}", [(fa, f"o{t}")], lambda e, b, t=t: e.dma_start(
                ov[bass.ds(b, 1), :, t, :].rearrange("a p n -> p (a n)"), nat[:, t, :]))
        with nc.Block() as block:
            @block.vector
            def _(e):
                fv.run(e, B)

            @block.tensor
            def _(e):
                fp.run(e, B)

            @block.scalar
            def _(e):
                fa.run(e, B)

            @block.sync
            def _(e):
                fs.run(e, B)
                for s in fs.sem:
                    e.wait_ge(s, (B + 1) * 16)


_INS = ['x', 'cond_2048', 'L0_cond_W_emb', 'L0_cond_b_emb', 'L0_cond_g_norm', 'L0_cond_W_qkv', 'L0_cond_g_q',
        'L0_cond_g_k', 'L0_cond_W_out', 'L1_cond_W_ih', 'L1_cond_W_hh', 'L1_cond_b_ih', 'L1_cond_b_hh', 'L3_cond_b']


def kernel(**inputs):
    import numpy as np
    import concourse.bacc as bacc
    from concourse.bass_utils import run_bass_kernel_spmd

    nc = bacc.Bacc("TRN2", target_bir_lowering=False, num_devices=1)
    arrays, args = {}, []
    for name in _INS:
        a = np.ascontiguousarray(inputs[name])
        arrays[f"in_{name}"] = a
        args.append(nc.dram_tensor(f"in_{name}", a.shape, mybir.dt.from_np(a.dtype), kind="ExternalInput").ap())
    args.append(nc.dram_tensor("out_0", (B, T, D), F32, kind="ExternalOutput").ap())
    build(nc, *args)
    r = run_bass_kernel_spmd(nc, [arrays], core_ids=[0])
    return r.results[0]["out_0"]
```

```python
import concourse.bass as bass
from concourse import mybir
from contextlib import ExitStack

F32 = mybir.dt.float32
ALU = mybir.AluOpType
ACT = mybir.ActivationFunctionType
AX = mybir.AxisListType

B, T, D, HEADS = 4, 512, 512, 16
P = 128
C = D // P
NG = 4
DH = D // HEADS
TAPS = B
PAD = TAPS - 1
TP = T + PAD
TB = T // P
NI = C * B
EPS = 1e-6


R_COND, R_GN, R_B3, R_BES, R_BEH, R_BI, R_BH, R_GQ, R_GK = 0, 4, 5, 6, 7, 8, 11, 14, 15


class Queue:

    def __init__(self, sem):
        self.sem, self.items, self.at, self.dmas = sem, [], {}, []

    def add(self, name, waits, fn, dmas=1):
        assert name not in self.at, name
        self.items.append((name, waits, fn))
        self.at[name] = len(self.items)
        self.dmas.append(dmas)

    def run(self, eng, passes, apart=None):
        if isinstance(self.sem, list):
            for sem, n in zip(self.sem, self.dmas):
                eng.sem_inc(sem, 16 * n)
        else:
            eng.sem_inc(self.sem, len(self.items))
        if passes == 1:
            self.one_pass(eng, 0, apart, alone=True)
        else:
            with eng.Fori(0, passes) as it:
                self.one_pass(eng, it, apart)

    def one_pass(self, eng, it, apart, alone=False):
        passed = {}
        for i, (name, waits, fn) in enumerate(self.items):
            for w in waits:
                q, other, before = w if len(w) == 3 else (*w, False)
                if other not in q.at or (alone and before):
                    continue
                n, total = q.at[other], len(q.items)
                if isinstance(q.sem, list):
                    sem, value = q.sem[n - 1], (it + (1 if before else 2)) * (16 * q.dmas[n - 1])
                else:
                    if before:
                        n -= total
                    if passed.get(id(q), -total) >= n:
                        continue
                    passed[id(q)] = n
                    sem, value = q.sem, it * total + (total + n)
                eng.wait_ge(sem, value)
                if apart is not None:
                    eng.sem_inc(apart, 1)
            done = fn(eng, it)
            if isinstance(self.sem, list):
                for d in done:
                    d.then_inc(self.sem[i], 16)
                assert len(done) == self.dmas[i]
            else:
                done.then_inc(self.sem, 1)


def regroup(src, dst):
    return (src.rearrange("p (g c j) -> p c g j", g=NG, c=C), dst.rearrange("p (c g j) -> p c g j", g=NG, c=C))


def load_rows(eng, dst, src):
    rows = src.rearrange("(g c j) n -> g j c n", g=NG, c=C)
    return [eng.dma_start(dst[32 * g:32 * g + 32], rows[g]) for g in range(NG)]


def build(nc, x, cond, W_emb, b_emb, g_norm, W_qkv, g_q, g_k, W_out, W_ih, W_hh, b_ih, b_hh, b3, out):
    with ExitStack() as ctx:
        def sb(name, shape):
            return ctx.enter_context(nc.sbuf_tensor(name, shape, F32))

        def sem(name):
            return ctx.enter_context(nc.semaphore(name))

        bank = [ctx.enter_context(nc.psum_tensor(f"bank{i}", [P, 512], F32)) for i in range(8)]

        whh = sb("whh", [P, C, 3 * D])
        seq = sb("seq", [P, NI, TP])
        ident = sb("ident", [P, P])
        vecT = sb("vecT", [P, C, 32])
        bias_g = sb("bias_g", [P, 3, C])
        tap = sb("tap", [P, TAPS, NI, 2])
        b3x = sb("b3x", [P, NI, 2])
        arena = sb("arena", [P, 3 * NI * (T + 1)])
        arena2 = sb("arena2", [P, NI * TP])
        gi = arena[:].rearrange("p (t i) -> p t i", i=3 * NI)
        seq2 = arena2[:].rearrange("p (i t) -> p i t", i=NI)
        wih = arena2[:, 0:C * 3 * D].rearrange("p (c n) -> p c n", c=C)

        at = [0]

        def take(n):
            at[0] += n
            assert at[0] <= 3 * NI * T
            return arena[:, at[0] - n:at[0]]

        wqkv = take(C * 3 * D).rearrange("p (c n) -> p c n", c=C)
        wout = take(C * D).rearrange("p (c n) -> p c n", c=C)
        x_nat = take(TB * D).rearrange("p (t n) -> p t n", t=TB)
        xp = take(TB * D).rearrange("p (t n) -> p t n", t=TB)
        xnT = take(C * T).rearrange("p (c t) -> p c t", c=C)
        v_nat = take(TB * D).rearrange("p (t n) -> p t n", t=TB)
        oT = take(C * T).rearrange("p (c t) -> p c t", c=C)
        kT = take(2 * T).rearrange("p (a t) -> p a t", a=2)
        qm = take(2 * NG * T).rearrange("p (a g t) -> p a g t", a=2, g=NG)
        qn = take(T)
        sqb = take(T)
        wemb = arena2[:, 0:C * 2 * D].rearrange("p (c n) -> p c n", c=C)
        stage = oT[:, 0, 0:P]
        rnb = sb("rnb", [P, T])
        pT = arena2[:, 0:NG * TB * T].rearrange("p (g b n) -> p g b n", g=NG, b=TB)
        NP = 8
        prob = sb("prob", [P, NP, T])
        small = sb("small", [P, 64])
        mn, sm, ri = small[:, 0:8], small[:, 8:16], small[:, 16:24]
        ssx, lnx, rsx = small[:, 24:28], small[:, 28:32], small[:, 32:36]
        cur = small[:, 36:44].rearrange("p (s c) -> p s c", s=2)
        eps = small[:, 44:45]
        maskn = small[:, 45:49]
        modT = sb("modT", [P, 2, C, B])
        ones = sb("ones", [P, P])

        xv = x.rearrange("b (t p) n -> b p t n", p=P)
        seq5 = seq[:].rearrange("p (h b c) t -> p h b c t", h=2, b=B)

        def seq_at(c, b):
            return seq5[:, c // 2, bass.ds(b, 1), c % 2, PAD:TP]

        NS, QK, SS, OB = 3, 5, 6, 7
        OBANK = [1, 4, 6, 5]
        LAG = 3
        NM = HEADS * TB
        MC = NG * TB
        wq = wqkv.rearrange("p k (s c n) -> p k s c n", s=3, c=C)
        wo = wout.rearrange("p k (c n) -> p k c n", c=C)

        def phase(name, batches, attend, prepare):
            qd = Queue([sem(f"{name}_load{i}") for i in range(4)])
            qw = Queue([sem(f"{name}_emb")])
            qa, qv, qg, qp = [Queue(sem(f"{name}_{q}")) for q in ("act", "dve", "pool", "pe")]
            first = batches[0]

            def following(b):
                return b + (first + 1)

            def own(b):
                return b + first

            def load_x():
                qd.add("x", [(qa, "xp3", True), (qa, "sq3", True)],
                        lambda e, b: [e.dma_start(x_nat, xv[bass.ds(following(b), 1)].rearrange("a p t n -> p (a t) n"))])

            def scale_now():
                qv.add("cur", [(qv, f"mod{C - 1}")], lambda e, b: e.tensor_copy(
                    cur, modT[:].rearrange("p s c b -> p (s c) b")[:, :, bass.ds(following(b), 1)]
                    .rearrange("p (s c) b -> p s (c b)", s=2)))

            def squares(t):
                qa.add(f"sq{t}", [(qd, "x"), (qa, f"sq{t - 1}" if t else "oe0")],
                       lambda e, b: e.activation(bank[OB][:], x_nat[:, t, :], ACT.Square, accum_out=ssx[:, t:t + 1]))
                if t == TB - 1:
                    qa.add("lnx", [(qa, "sq3"), (qv, "eps")], lambda e, b: e.activation(lnx, ssx, ACT.Ln, bias=eps, scale=1.0 / D))
                    qa.add("rsx", [(qa, "lnx")], lambda e, b: e.activation(rsx, lnx, ACT.Exp, scale=-0.5))

            def group(t):
                def copy(e, b):
                    src, dst = regroup(x_nat[:, t, :], xp[:, t, :])
                    return e.activation(dst, src, ACT.Copy)
                qa.add(f"xp{t}", [(qd, "x"), (qg, "o23", True)], copy)

            def transposes(e, dst, c):
                for t in range(TB):
                    last = e.transpose(dst[:, 128 * t:128 * t + 128], xp[:, t, 128 * c:128 * c + 128], ident[:])
                return last

            def turn_x(c):
                prior = (qa, f"xr{c - 2}") if c >= 2 else ((qv, "kn3"), (qa, "kl3"))[c]
                qp.add(f"tx{c}", [(qa, "xp3"), (qg, "ident"), prior], lambda e, b: transposes(e, bank[5 + c % 2], c))
                qa.add(f"xr{c}", [(qp, f"tx{c}")],
                       lambda e, b: e.activation(seq_at(c, following(b)),
                                                 bank[5 + c % 2][:].rearrange("p (a t) -> p a t", a=1), ACT.Copy))

            def scale_x(t):
                qv.add(f"xn{t}", [(qa, "rsx"), (qp, "tx3")],
                       lambda e, b: e.tensor_scalar(xp[:, t, :], xp[:, t, :], rsx[:, t:t + 1], None, ALU.mult))

            def turn_xn(c):
                qp.add(f"tn{c}", [(qv, "xn3"), (qv, f"xt{c - 2}") if c >= 2 else (qa, f"xr{c + 2}")],
                       lambda e, b: transposes(e, bank[5 + c % 2], c))
                qv.add(f"xt{c}", [(qp, f"tn{c}"), (qp, "k3"), (qv, "cur")],
                       lambda e, b: e.tensor_scalar(xnT[:, c, :], bank[5 + c % 2][:], cur[:, 0, c:c + 1],
                                                    cur[:, 1, c:c + 1], ALU.mult, ALU.add))

            def project_v(t):
                def vproj(e, b):
                    for k in range(C):
                        last = e.matmul(bank[OB][:], xnT[:, k, 128 * t:128 * t + 128], wqkv[:, k, 2 * D:3 * D],
                                        start=k == 0, stop=k == C - 1)
                    return last
                qp.add(f"v{t}", [(qa, f"ve{t - 1}") if t else (qa, "oe3", True)], vproj)
                qa.add(f"ve{t}", [(qp, f"v{t}"), (qp, "pv3", True)],
                       lambda e, b: e.activation(v_nat[:, t, :], bank[OB][:], ACT.Copy))

            def tiles_done(c):
                return (qp, f"S{MC * (c - 2) + MC - 1}") if c >= 2 else (
                    (qp, f"S{NM - 1}", True) if c else (qp, f"S{3 * MC - 1}"))

            def pbank(s):
                return QK if attend or s == 0 else OB

            def norm_start(s, c):
                n = "qk"[s]
                prior = (qv, f"qn{c}" if attend else "xt3") if s else ((qv, "xt3"), (qv, "o13", True), (qv, "kn1"), (qv, "kn2"))[c]

                def proj(e, b):
                    for k in range(C):
                        last = e.matmul(bank[pbank(s)][:], wq[:, k, s, c], xnT[:, k, :], start=k == 0, stop=k == C - 1)
                    return last
                read = (qp, f"qs{c}") if s else ((qp, "ks3"), (qp, "ks0", True), (qp, "ks1"), (qp, "ks2"))[c]
                qp.add(f"{n}{c}", [prior, (qa, f"rg{6 + s}"), (qv, f"rg{6 + s}"), (qa, f"rg{9 + s}"), (qv, f"rg{9 + s}")], proj)
                qa.add(f"{n}2{c}", [(qp, f"{n}{c}"), read],
                       lambda e, b: e.activation(sqb, bank[pbank(s)][:], ACT.Square))

            def norm_end(s, c):
                n = "qk"[s]
                prior = (qa, f"ql{c}") if s else ((qv, "xt3"), (qv, "o12", True), (qa, "kl1"), (qa, "kl2"))[c]
                qp.add(f"{n}s{c}", [(qa, f"{n}2{c}"), (qv, f"ones{NG - 1}"), prior],
                       lambda e, b: e.matmul(bank[SS][:], ones[:], sqb, start=True, stop=True))
                used = (qv, f"qn{c}") if s else ((qv, "kn3"), (qv, "kn0", True), (qv, "kn1"), (qv, "kn2"))[c]
                qa.add(f"{n}l{c}", [(qp, f"{n}s{c}"), used],
                       lambda e, b: e.activation(rnb[:], bank[SS][:], ACT.Ln, bias=eps, scale=1.0 / DH))
                qa.add(f"{n}r{c}", [(qa, f"{n}l{c}")],
                       lambda e, b: e.activation(rnb[:], rnb[:], ACT.Exp, scale=-0.5))

            def norm_apply(s, c):
                if s == 0:
                    masked = ((qg, "qm33"), (qg, "qm03", True), (qg, "qm13"), (qg, "qm23"))[c]
                    qv.add(f"qn{c}", [(qa, f"qr{c}"), masked],
                           lambda e, b: e.scalar_tensor_tensor(qn, bank[pbank(s)][:], vecT[:, 0, R_GQ:R_GQ + 1], rnb[:],
                                                               ALU.mult, ALU.mult))
                else:
                    qv.add(f"kn{c}", [(qa, f"kr{c}"), tiles_done(c)],
                           lambda e, b: e.scalar_tensor_tensor(kT[:, c % 2, :], bank[pbank(s)][:], vecT[:, 0, R_GK:R_GK + 1],
                                                               rnb[:], ALU.mult, ALU.mult))

            def mask(c, g):
                qg.add(f"qm{c}{g}", [(qv, f"qn{c}"), (qv, f"maskn{NG - 1}"), tiles_done(c)],
                       lambda e, b: e.tensor_scalar(qm[:, c % 2, g, :], qn, maskn[:, g:g + 1], 1.0,
                                                    ALU.mult, ALU.mult))

            def before(q, name, m, n):
                return (q, f"{name}{m - n}") if m >= n else (q, f"{name}{NM + m - n}", True)

            def slot(m):
                return slice(m % NP, m % NP + 1)

            def products(m):
                c, g, t = m // MC, m // TB % NG, m % TB
                free = (qa, f"e{m - NS}") if m >= NS else (qv, "o10", True) if m == 1 else (qa, f"e{NM - 1}", True)
                qp.add(f"S{m}", [(qg, f"qm{c}3", c == 0), (qv, f"kn{c}", c == 0), free],
                       lambda e, b: e.matmul(bank[m % NS][:], qm[:, c % 2, g, 128 * t:128 * t + 128], kT[:, c % 2, :],
                                             start=True, stop=True))
                qv.add(f"mn{m}", [(qp, f"S{m}"), before(qa, "e", m, NP)],
                       lambda e, b: e.tensor_reduce(mn[:, slot(m)], bank[m % NS][:], AX.X, ALU.min))

            def exponentials(m):
                qa.add(f"e{m}", [(qv, f"mn{m}"), before(qp, "T", m, NP), before(qv, "ri", m, NP)],
                       lambda e, b: e.activation(prob[:, m % NP, :], bank[m % NS][:], ACT.Exp, bias=mn[:, slot(m)],
                                                 scale=-1.0, accum_out=sm[:, slot(m)]))

            def normalise(m):
                qv.add(f"ri{m}", [(qa, f"e{m}"), before(qg, "n", m, NP)],
                       lambda e, b: e.reciprocal(ri[:, slot(m)], sm[:, slot(m)]))
                qg.add(f"n{m}", [(qv, f"ri{m}")],
                       lambda e, b: e.tensor_scalar(prob[:, m % NP, :], prob[:, m % NP, :], ri[:, slot(m)], 1.0,
                                                    ALU.mult, ALU.mult))

            def turn(m):
                g, t = m // TB % NG, m % TB
                dst = bank[3 + m % 2]

                def tr(e, b):
                    for k in range(TB):
                        last = e.transpose(dst[:, 128 * k:128 * k + 128], prob[:, m % NP, 128 * k:128 * k + 128],
                                           ident[:])
                    return last
                qe = (qa, qv)[m % 2]
                prior = (qe, f"p{m - 2}") if m >= 2 else ((qv, "o11", True) if m else (qa, f"p{NM - 2}", True))
                qp.add(f"T{m}", [(qg, f"n{m}"), prior], tr)
                free = (qp, f"pv{m // MC - 1}") if m >= MC else (qp, "pv3", True)
                if m % 2 == 0:
                    qa.add(f"p{m}", [(qp, f"T{m}"), free], lambda e, b: e.activation(pT[:, g, t, :], dst[:], ACT.Copy))
                else:
                    qv.add(f"p{m}", [(qp, f"T{m}"), free], lambda e, b: e.tensor_copy(pT[:, g, t, :], dst[:]))

            def values(c):
                def pv(e, b):
                    for k in range(TB):
                        for g in range(NG):
                            last = e.matmul(bank[OB][32 * g:32 * g + DH, :],
                                            v_nat[:, k, 128 * c + 32 * g:128 * c + 32 * g + DH],
                                            pT[:, g, :, 128 * k:128 * k + 128], start=k == 0, stop=k == TB - 1)
                    return last
                qp.add(f"pv{c}", [(qa, f"p{MC * c + MC - 2}"), (qv, f"p{MC * c + MC - 1}"), (qa, "ve3"),
                                  (qa, f"oe{c - 1}" if c else "ve3"), (qa, "sq3" if c else "ve3")], pv)
                qa.add(f"oe{c}", [(qp, f"pv{c}"), (qv, "o13", True)],
                       lambda e, b: e.activation(oT[:, c, :], bank[OB][:], ACT.Copy))

            def oproj(c, chunks):
                def products(e, b):
                    for k in chunks:
                        last = e.matmul(bank[OBANK[c]][:], wo[:, k, c], oT[:, k, :], start=k == 0, stop=k == C - 1)
                    return last
                return products

            def project_o_early(c):
                prior = ((qa, f"e{NM - 1}"), (qv, f"p{NM - 1}"))[c]
                qp.add(f"op{c}early", [(qa, "oe2"), prior], oproj(c, range(C - 1)))

            def project_o(c):
                prior = [[], [], [(qa, "kl0"), (qa, "kl3")], [(qv, "kn0"), (qv, "kn3")]][c]
                qp.add(f"op{c}", [(qa, "oe3")] + prior, oproj(c, range(C - 1 if c < 2 else 0, C)))
                tmp = xp[:, c, :]
                qv.add(f"o1{c}", [(qp, f"op{c}"), (qg, f"o2{c}", True)],
                       lambda e, b: e.tensor_tensor(tmp, bank[OBANK[c]][:], oT[:, c, :], ALU.add))
                qg.add(f"o2{c}", [(qv, f"o1{c}"), (qa, f"xr{c}", True)],
                       lambda e, b: e.tensor_tensor(seq_at(c, own(b)), seq_at(c, own(b)),
                                                    tmp.rearrange("p (a t) -> p a t", a=1), ALU.add))

            sT = oT[:, 1, 0:256].rearrange("p (q c i) -> p q c i", q=2, c=C)

            def clear():
                qv.add("stage", [], lambda e, b: e.memset(stage, 0.0))
                qv.add("bank0", [], lambda e, b: e.memset(bank[0][:, 0:256], 0.0))
                qv.add("ones", [], lambda e, b: e.memset(ones[:], 0.0))
                qv.add("maskn", [], lambda e, b: e.memset(maskn, 0.0))
                qv.add("eps", [], lambda e, b: e.memset(eps, EPS))
                for g in range(NG):
                    q = slice(32 * g, 32 * g + 32)
                    qv.add(f"ones{g}", [(qv, "ones")], lambda e, b, q=q: e.memset(ones[q, q], 1.0))
                    qv.add(f"maskn{g}", [(qv, "maskn")],
                           lambda e, b, q=q, g=g: e.memset(maskn[q, g:g + 1], -float(DH) ** -0.5))
                qg.add("ident0", [], lambda e, b: e.memset(ident[:], 0.0))
                qg.add("ident", [(qg, "ident0")], lambda e, b: e.affine_select(
                    out=ident[:], in_=ident[:], compare_op=ALU.not_equal, fill=1.0, base=0,
                    pattern=[[-1, P]], channel_multiplier=1))
                qg.add("pad", [], lambda e, b: e.memset(seq[:, :, 0:PAD], 0.0))

            def load_weights():
                qd.add("wqkv", [], lambda e, b: load_rows(e, whh[:], W_qkv), NG)
                qd.add("wout", [], lambda e, b: load_rows(e, v_nat, W_out), NG)

            def load_vectors():
                def load(e, b):
                    many = [(R_COND + i, cond[i, :]) for i in range(B)] + [(R_GN, g_norm), (R_B3, b3)]
                    many += [(R_BES + q, b_emb[q * D:q * D + D]) for q in range(2)]
                    many += [(R_BI + q, b_ih[q * D:q * D + D]) for q in range(3)]
                    many += [(R_BH + q, b_hh[q * D:q * D + D]) for q in range(3)]
                    done = [e.dma_start(stage[r:P:32, :], v.rearrange("(g n) -> g n", g=NG)) for r, v in many]
                    for g in range(NG):
                        for r, v in ((R_GQ, g_q), (R_GK, g_k)):
                            done.append(e.dma_start(stage[32 * g + r:32 * g + r + 1, 0:DH],
                                                    v.rearrange("(a n) -> a n", a=1)))
                    return done
                qd.add("vec", [(qv, "stage")], load, B + 10 + 2 * NG)
                qv.add("vecT", [(qd, "vec")], lambda e, b: e.transpose(
                    vecT[:], stage.rearrange("p (c i) -> p c i", c=C)))

            def modulation():
                wv = wemb.rearrange("p c (q G n) -> p c q G n", q=2, G=NG)

                def emb(e, b):
                    for k in range(C):
                        for G in range(NG):
                            last = e.matmul(bank[0][32 * G:32 * G + B, 0:256], vecT[:, k, 0:B], wv[:, k, :, G, :],
                                            start=k == 0, stop=k == C - 1)
                    return last
                qp.add("emb", [(qw, "wemb"), (qv, "vecT"), (qv, "bank0")], emb)
                qv.add("sT", [(qp, "emb")], lambda e, b: e.transpose(
                    sT, bank[0][:, 0:256].rearrange("p (q c i) -> p q c i", q=2, c=C)))
                for c in range(C):
                    qv.add(f"scale{c}", [(qv, "sT")], lambda e, b, c=c: e.tensor_scalar(
                        modT[:, 0, c, :], sT[:, 0, c, 0:B], vecT[:, c, R_BES:R_BES + 1], 1.0, ALU.add, ALU.add))
                    qv.add(f"shift{c}", [(qv, "sT")], lambda e, b, c=c: e.tensor_scalar(
                        modT[:, 1, c, :], sT[:, 1, c, 0:B], vecT[:, c, R_BEH:R_BEH + 1], None, ALU.add))
                for c in range(C):
                    qv.add(f"mod{c}", [(qv, f"scale{c}")], lambda e, b, c=c: e.tensor_scalar(
                        modT[:, 0, c, :], modT[:, 0, c, :], vecT[:, c, R_GN:R_GN + 1], None, ALU.mult))

            def regroup_all(name, src, dst, queues, waits, order):
                for i in order:
                    a, d = regroup(src[:, i * D:i * D + D], dst[:, i * D:i * D + D])
                    if queues[i % len(queues)] is qa:
                        qa.add(f"{name}{i}", waits, lambda e, b, a=a, d=d: e.activation(d, a, ACT.Copy))
                    else:
                        qv.add(f"{name}{i}", waits, lambda e, b, a=a, d=d: e.tensor_copy(d, a))

            def flat(v):
                return v.rearrange("p c n -> p (c n)")

            def spread_vectors():
                for q in range(2):
                    qv.add(f"bias{q}", [(qv, "vecT")], lambda e, b, q=q: e.tensor_tensor(
                        bias_g[:, q, :], vecT[:, :, R_BI + q], vecT[:, :, R_BH + q], ALU.add))
                qv.add("bias2", [(qv, "vecT")], lambda e, b: e.tensor_copy(bias_g[:, 2, :], vecT[:, :, R_BI + 2]))
                for i in range(0, NI, 2):
                    for s in range(2):
                        cs = slice(2 * (i // 8), 2 * (i // 8) + 2)
                        qv.add(f"tap{i}{s}", [], lambda e, b, i=i, s=s, cs=cs: e.tensor_copy(
                            tap[:, :, i:i + 2, s], vecT[:, cs, 0:TAPS].rearrange("p c k -> p k c")))
                        qv.add(f"b3{i}{s}", [], lambda e, b, i=i, s=s, cs=cs: e.tensor_copy(
                            b3x[:, i:i + 2, s], vecT[:, cs, R_B3]))

            if not attend:
                clear()
                qw.add("wemb", [], lambda e, b: load_rows(e, wemb, W_emb), NG)
                load_x()
                load_vectors()
                load_weights()
                for t in range(TB):
                    squares(t)
                for t in range(TB):
                    group(t)
                for c in range(C):
                    turn_x(c)
                for t in range(TB):
                    scale_x(t)
                modulation()
                scale_now()
                for c in range(C):
                    turn_xn(c)
                for s in range(2):
                    regroup_all("rg", flat(whh), flat(wqkv), (qa, qv), [(qd, "wqkv")], range(s, 3 * C, 3))
                regroup_all("wo", flat(v_nat), flat(wout), (qv,), [(qd, "wout")], range(C))
                spread_vectors()
                norm_start(0, 0)
                norm_start(1, 0)
                regroup_all("rg", flat(whh), flat(wqkv), (qv,), [(qd, "wqkv")], range(2, 3 * C, 3))
                for s in range(2):
                    norm_end(s, 0)
                    norm_apply(s, 0)
                for g in range(NG):
                    mask(0, g)
            if attend and prepare:
                load_x()
                scale_now()
            beside = {m: [] for m in range(NM + LAG + 1)}
            if attend:
                for c in range(1, C):
                    m = MC * (c - 1)
                    for off, f, s in ((1, norm_start, 0), (4, norm_end, 0), (5, norm_apply, 0),
                                      (7, norm_start, 1), (10, norm_end, 1), (11, norm_apply, 1)):
                        beside[m + off].append((f, s, c))
                    for g in range(NG):
                        beside[m + 6 + g].append((mask, c, g))
                for t in range(TB):
                    beside[2 + 4 * t].append((project_v, t))
                beside[NM + 1].append((project_o_early, 0))
            if attend and prepare:
                for t in range(TB):
                    beside[24 + t].append((squares, t))
                    beside[37 + t].append((group, t))
                    beside[45 + t].append((turn_x, t))
                    beside[49 + t // 2].append((scale_x, t))
                    beside[52 + t].append((turn_xn, t))
                for m, f, s in ((56, norm_start, 0), (59, norm_end, 0), (60, norm_apply, 0),
                                (NM, norm_start, 1), (NM + LAG, norm_end, 1), (NM + LAG, norm_apply, 1)):
                    beside[m].append((f, s, 0))
                for g in range(NG):
                    beside[61 + g].append((mask, 0, g))
            if attend:
                beside[NM + LAG].append((project_o_early, 1))
            for m in range(NM + LAG + 1):
                if attend:
                    if m < NM:
                        products(m)
                    if LAG <= m < NM + LAG:
                        turn(m - LAG)
                    if m > LAG and m % MC == LAG:
                        values(m // MC - 1)
                    if m < NM:
                        exponentials(m)
                    if 1 <= m <= NM:
                        normalise(m - 1)
                for f, *args in beside[m]:
                    f(*args)
            if attend and not prepare:
                qd.add("wih", [(qp, "k3")], lambda e, b: load_rows(e, wqkv, W_ih), NG)
                regroup_all("ih", flat(wqkv), flat(wih), (qa, qv), [(qd, "wih"), (qp, "pv3")], range(3 * C))
            if attend:
                for c in range(C):
                    project_o(c)

            passes = len(batches)
            with nc.Block() as block:
                @block.sync
                def _(e):
                    if attend and prepare:
                        for d in load_rows(e, whh[:], W_hh):
                            d.then_inc(s_whh, 16)
                    qd.run(e, passes)
                    if not prepare:
                        e.wait_ge(s_whh, NG * 16)

                @block.scalar
                def _(e):
                    e.preload_act_table_set("natural_log_exp_and_others")
                    qw.run(e, passes)
                    qa.run(e, passes)

                @block.vector
                def _(e):
                    qv.run(e, passes)

                @block.gpsimd
                def _(e):
                    qg.run(e, passes, apart=s_apart)

                @block.tensor
                def _(e):
                    qp.run(e, passes)

        s_whh = sem("s_whh")
        s_apart = sem("s_apart")
        phase("first", [-1], attend=False, prepare=True)
        phase("most", list(range(B - 1)), attend=True, prepare=True)
        phase("last", [B - 1], attend=True, prepare=False)

        ga, gv, gp = Queue(sem("gi_act")), Queue(sem("gi_dve")), Queue(sem("gi_pe"))
        wi = wih.rearrange("p k (q c n) -> p k q c n", q=3, c=C)
        gi6 = arena[:, 0:3 * NI * T].rearrange("p (t q h b c) -> p t q h b c", q=3, h=2, b=B, c=2)
        for i in range(3 * C):
            q, c = i // C, i % C

            def prod(e, b, i=i, q=q, c=c):
                for k in range(C):
                    last = e.matmul(bank[i % 6][:], wi[:, k, q, c], seq_at(k, b), start=k == 0, stop=k == C - 1)
                return last
            qe = (ga, gv)[i % 2]
            gp.add(f"g{i}", [(qe, f"g{i - 6}") if i >= 6 else (qe, f"g{i + 6}", True)], prod)
            dst = gi6[:, :, q, c // 2, :, c % 2]
            if i % 2 == 0:
                ga.add(f"g{i}", [(gp, f"g{i}")], lambda e, b, i=i, q=q, c=c, dst=dst: e.activation(
                    dst[:, :, bass.ds(b, 1)], bank[i % 6][:].rearrange("p (t a) -> p t a", a=1), ACT.Identity,
                    bias=bias_g[:, q, c:c + 1]))
            else:
                gv.add(f"g{i}", [(gp, f"g{i}")], lambda e, b, i=i, q=q, c=c, dst=dst: e.tensor_scalar(
                    dst[:, :, bass.ds(b, 1)], bank[i % 6][:].rearrange("p (t a) -> p t a", a=1),
                    bias_g[:, q, c:c + 1], None, ALU.add))
        with nc.Block() as block:
            @block.tensor
            def _(e):
                gp.run(e, B)

            @block.scalar
            def _(e):
                ga.run(e, B)

            @block.vector
            def _(e):
                gv.run(e, B)

        used = [0]
        prob_flat = prob[:].rearrange("p a t -> p (a t)")

        def tile(shape):
            n = 1
            for d in shape[1:]:
                n *= d
            used[0] += n
            assert used[0] <= NP * T
            v = prob_flat[:, used[0] - n:used[0]]
            return v if len(shape) == 2 else v.rearrange("p (a b) -> p a b", a=shape[1])

        hb = tile([P, 2, 4 * NI])
        tr_rz = tile([P, 2, P])
        gate_in = tile([P, 2 * NI])
        gin = tile([P, 2, 2 * NI])
        r_d0 = tile([P, 3 * NI])
        n_d1 = tile([P, 2, 3 * 64])
        scA = tile([P, 3 * NI])
        m_d0 = tile([P, 4 * NI])
        z_d1 = tile([P, 4 * NI])
        prd = tile([P, 2, TAPS * NI * 2])
        st = {n: sem(n) for n in ("s_clear", "s_h", "s_rz", "s_n", "s_tr", "s_sum", "s_sig", "s_pre", "s_gi",
                                  "s_tanh", "s_x3", "s_pool")}
        RZ, BN = ((0, 0), (1, 2)), (3, 4)
        N_CLEAR = 10 + 1 + 2 + 2 * B + 2

        def every(ap, n):
            return ap.rearrange("p (i s) -> p i s", s=n)

        def of_half(tile_, h, w):
            return tile_[:, w * h:w * h + w]

        OB0, NOB, NNAT = 5, 3, 6
        POOL_OPS = 9
        nat = arena[:, 0:NNAT * D].rearrange("p (i n) -> p i n", i=NNAT)
        units = [(i // B, i % B) for i in range(TB * B)]
        s_turned = sem("out_turned")
        s_nat = (sem("out_nat_act"), sem("out_nat_dve"))
        s_store = [sem(f"out_store{i}") for i in range(NNAT)]

        def out_turn(e):
            for i, (t, b) in enumerate(units):
                if b == 0:
                    e.wait_ge(st["s_pool"], POOL_OPS * (P // 2) * (t + 1))
                if i >= NOB:
                    e.wait_ge(s_nat[(i - NOB) % 2], (i - NOB) // 2 + 1)
                for c in range(C):
                    last = e.transpose(
                        bank[OB0 + i % NOB][:].rearrange("p (g c j) -> p g c j", g=NG, c=C)[:, :, c, :],
                        seq5[:, c // 2, b, c % 2, P * t:P * t + P], ident[:])
                last.then_inc(s_turned, 1)

        def out_copy(e, odd, copy):
            for i in range(odd, len(units), 2):
                if i >= NNAT:
                    e.wait_ge(s_store[i % NNAT], 16 * (i // NNAT))
                e.wait_ge(s_turned, i + 1)
                copy(nat[:, i % NNAT, :], bank[OB0 + i % NOB][:]).then_inc(s_nat[odd], 1)

        def out_store(e):
            for i, (t, b) in enumerate(units):
                e.wait_ge(s_nat[i % 2], i // 2 + 1)
                e.dma_start(out[b, P * t:P * t + P, :], nat[:, i % NNAT, :]).then_inc(s_store[i % NNAT], 16)
            for i in range(NNAT):
                e.wait_ge(s_store[i], 16 * len(range(i, len(units), NNAT)))

        with nc.Block() as block:
            @block.sync
            def _(e):
                out_store(e)

            @block.vector
            def _(e):
                c = st["s_clear"]
                for v in (r_d0[:], m_d0[:], n_d1[:], bank[0][:, 0:P], bank[1][:, 0:P], bank[2][:, 0:P],
                          bank[3][:, 0:64], bank[4][:, 0:64], seq2[:, :, 0:PAD], gi[:, T, :]):
                    e.memset(v, 0.0).then_inc(c, 1)
                e.memset(z_d1[:], -1.0).then_inc(c, 1)
                e.wait_ge(c, 11)
                e.memset(every(z_d1[:], 4)[:, :, 0], 0.0).then_inc(c, 1)
                e.memset(every(r_d0[:], 3)[:, :, 1], 1.0).then_inc(c, 1)
                for h in range(2):
                    for b in range(B):
                        e.tensor_copy(n_d1[:, h, 6 * b:6 * b + 6].rearrange("p (i s) -> p i s", s=3)[:, :, 1],
                                      vecT[:, 2 * h:2 * h + 2, R_BH + 2]).then_inc(c, 1)
                for h in range(2):
                    src = vecT[:, 2 * h:2 * h + 2, 0:B].rearrange("p c b -> p b c")
                    dst = [of_half(v, h, 2 * NI).rearrange("p (b c s) -> p b c s", b=B, c=2)
                           for v in (hb[:, 0, :], m_d0)]
                    e.tensor_copy(dst[0][:, :, :, 3], src)
                    e.tensor_copy(dst[1][:, :, :, 2], src).then_inc(c, 1)
                e.wait_ge(c, N_CLEAR)
                with e.Fori(0, T // 2) as it:
                    for u in range(2):
                        t = it * 2 + u
                        t1 = e.snap(t + 1)
                        half = (e.snap(2 * t + 1), e.snap(2 * t + 2))
                        turned = [e.snap(4 * t + i) for i in (1, 2, 3, 4)]
                        h4 = e.snap(2 * t + 4)
                        now = e.snap(t + PAD)
                        def turn_rz(h):
                            e.wait_ge(st["s_rz"], half[h])
                            e.transpose(tr_rz[:, h, :].rearrange("p (q i c) -> p q c i", c=2, q=2),
                                        bank[RZ[h][u]][:, 0:P].rearrange("p (q c i) -> p q c i", q=2, c=2)
                                        ).then_inc(st["s_tr"], 1)

                        def add_input(h):
                            e.wait_ge(st["s_tr"], turned[(0, 2)[h]])
                            e.tensor_tensor(of_half(gate_in, h, NI).rearrange("p (q i) -> p q i", q=2),
                                            tr_rz[:, h, :].rearrange("p (q i) -> p q i", q=2)[:, :, 0:8],
                                            gin[:, u, :].rearrange("p (q h i) -> p h q i", q=2, h=2)[:, h],
                                            ALU.add).then_inc(st["s_sum"], 1)

                        def turn_n(h):
                            e.wait_ge(st["s_n"], half[h])
                            e.transpose(n_d1[:, h, :].rearrange("p (i c s) -> p c i s", c=2, s=3)[:, :, :, 0],
                                        bank[BN[h]][:, 0:64].rearrange("p (c i) -> p c i", c=2)
                                        ).then_inc(st["s_tr"], 1)

                        def scan_a(h):
                            e.wait_ge(st["s_tr"], turned[(1, 3)[h]])
                            e.wait_ge(st["s_sig"], half[h])
                            e.tensor_tensor_scan(of_half(scA, h, 24), of_half(r_d0, h, 24), n_d1[:, h, 0:24], 0.0,
                                                 ALU.mult, ALU.add).then_inc(st["s_pre"], 1)

                        def scan_b(h):
                            e.wait_ge(st["s_tanh"], half[h])
                            e.tensor_tensor_scan(of_half(hb[:, 1 - u, :], h, 2 * NI), of_half(m_d0, h, 2 * NI),
                                                 of_half(z_d1, h, 2 * NI), 0.0, ALU.subtract, ALU.mult
                                                 ).then_inc(st["s_h"], 1)

                        turn_rz(0)
                        e.wait_ge(st["s_gi"], t1)
                        add_input(0)
                        turn_n(0)
                        scan_a(0)
                        turn_rz(1)
                        scan_b(0)
                        add_input(1)
                        turn_n(1)
                        scan_a(1)
                        scan_b(1)
                        e.wait_ge(st["s_h"], h4)
                        e.tensor_tensor(seq[:, :, bass.ds(now, 1)], seq[:, :, bass.ds(now, 1)],
                                        every(hb[:, 1 - u, :], 4)[:, :, 3:4], ALU.add).then_inc(st["s_x3"], 1)
                out_copy(e, 1, lambda d, s: e.tensor_copy(d, s))

            @block.scalar
            def _(e):
                e.wait_ge(st["s_clear"], N_CLEAR)
                e.preload_act_table_set("sigmoid_and_others")
                n_in = n_d1[:, :, 0:24].rearrange("p h (i s) -> p h i s", s=3)[:, :, :, 2]
                e.sem_inc(st["s_h"], 2)

                def bring(t, u):
                    e.activation(gin[:, u:u + 1, :], gi[:, bass.ds(t, 1), 0:2 * NI], ACT.Copy)
                    e.activation(n_in, gi[:, bass.ds(t, 1), 2 * NI:3 * NI].rearrange("p a (h i) -> p (a h) i", h=2),
                                 ACT.Copy).then_inc(st["s_gi"], 1)
                bring(0, 0)
                with e.Fori(0, T // 2) as it:
                    for u in range(2):
                        t = it * 2 + u
                        half = (e.snap(2 * t + 1), e.snap(2 * t + 2))
                        h4, following = e.snap(2 * t + 4), e.snap(t + 1)
                        for h in range(2):
                            e.wait_ge(st["s_sum"], half[h])
                            e.activation(every(of_half(r_d0, h, 24), 3)[:, :, 2], of_half(gate_in, h, NI)[:, 0:8],
                                         ACT.Sigmoid).then_inc(st["s_sig"], 1)
                            e.activation(every(of_half(z_d1, h, 2 * NI), 4)[:, :, 2], of_half(gate_in, h, NI)[:, 8:16],
                                         ACT.Sigmoid)
                            e.wait_ge(st["s_pre"], half[h])
                            pre = every(of_half(scA, h, 24), 3)[:, :, 2:3]
                            dst = of_half(m_d0, h, 2 * NI).rearrange("p (i a s) -> p i a s", a=2, s=2)
                            e.activation(dst[:, :, :, 1], pre.broadcast_to([P, 8, 2]), ACT.Tanh, scale=-1.0
                                         ).then_inc(st["s_tanh"], 1)
                        bring(following, 1 - u)
                        e.wait_ge(st["s_h"], h4)
                        e.activation(every(m_d0[:], 4)[:, :, 2], every(hb[:, 1 - u, :], 4)[:, :, 3], ACT.Copy)
                out_copy(e, 0, lambda d, s: e.activation(d, s, ACT.Copy))

            @block.tensor
            def _(e):
                e.wait_ge(st["s_clear"], N_CLEAR)
                wv = whh[:].rearrange("p c (q G n) -> p c q G n", q=3, G=NG)
                with e.Fori(0, T // 2) as it:
                    for u in range(2):
                        t = it * 2 + u
                        half = (e.snap(2 * t + 1), e.snap(2 * t + 2))
                        hv = hb[:, u, :].rearrange("p (h b c s) -> p h b c s", h=2, c=2, s=4)

                        def products(dst, gates, h, chunks):
                            n = (gates.stop - gates.start) * 64
                            for k in chunks:
                                for G in range(NG):
                                    last = e.matmul(bank[dst][32 * G:32 * G + B, 0:n], hv[:, k // 2, :, k % 2, 3],
                                                    wv[:, k, gates, G, 64 * h:64 * h + 64],
                                                    start=k == 0, stop=k == C - 1)
                            return last
                        rz, n = slice(0, 2), slice(2, 3)
                        e.wait_ge(st["s_h"], half[0])
                        products(RZ[0][u], rz, 0, (0, 1))
                        products(BN[0], n, 0, (0, 1))
                        products(RZ[1][u], rz, 1, (0,))
                        e.wait_ge(st["s_h"], half[1])
                        products(RZ[0][u], rz, 0, (2, 3)).then_inc(st["s_rz"], 1)
                        products(BN[0], n, 0, (2, 3)).then_inc(st["s_n"], 1)
                        products(RZ[1][u], rz, 1, (1, 2, 3)).then_inc(st["s_rz"], 1)
                        products(BN[1], n, 1, range(C)).then_inc(st["s_n"], 1)
                out_turn(e)

            @block.gpsimd
            def _(e):
                e.wait_ge(st["s_clear"], N_CLEAR)
                s = st["s_pool"]

                def wait(sem_, n):
                    e.wait_ge(sem_, n)
                    e.sem_inc(s_apart, 1)
                with e.Fori(0, T // 2) as it:
                    t = e.snap(it * 2)
                    t3 = e.snap(it * 2 + PAD)
                    wait(st["s_x3"], it * 2 + 2)

                    def conv(src, n):
                        for k in range(TAPS):
                            w = 2 * NI
                            last = e.tensor_tensor(prd[:, 0, w * k:w * k + w].rearrange("p (i s) -> p i s", s=2),
                                                   tap[:, k], src[:, :, bass.ds(t + k, 2)], ALU.mult)
                        last.then_inc(s, 1)
                        wait(s, it * POOL_OPS + n)
                        e.tensor_tensor(prd[:, 1, 0:64], prd[:, 0, 0:64], prd[:, 0, 64:128], ALU.add).then_inc(s, 1)
                        wait(s, it * POOL_OPS + n + 1)
                        e.tensor_tensor(prd[:, 1, 64:96], prd[:, 1, 0:32], prd[:, 1, 32:64], ALU.add).then_inc(s, 1)
                        wait(s, it * POOL_OPS + n + 2)
                    part = prd[:, 1, 64:96].rearrange("p (i s) -> p i s", s=2)
                    conv(seq, 1)
                    e.tensor_tensor(seq2[:, :, bass.ds(t3, 2)], seq[:, :, bass.ds(t3, 2)], part, ALU.add).then_inc(s, 1)
                    wait(s, it * POOL_OPS + 4)
                    conv(seq2, 5)
                    e.tensor_tensor(prd[:, 1, 96:128].rearrange("p (i s) -> p i s", s=2), part, b3x[:], ALU.add).then_inc(s, 1)
                    wait(s, it * POOL_OPS + 8)
                    e.tensor_tensor(seq[:, :, bass.ds(t, 2)], seq2[:, :, bass.ds(t3, 2)],
                                    prd[:, 1, 96:128].rearrange("p (i s) -> p i s", s=2), ALU.add).then_inc(s, 1)
                    wait(s, it * POOL_OPS + 9)


_INS = ['x', 'cond_2048', 'L0_cond_W_emb', 'L0_cond_b_emb', 'L0_cond_g_norm', 'L0_cond_W_qkv', 'L0_cond_g_q',
        'L0_cond_g_k', 'L0_cond_W_out', 'L1_cond_W_ih', 'L1_cond_W_hh', 'L1_cond_b_ih', 'L1_cond_b_hh', 'L3_cond_b']


def kernel(**inputs):
    import numpy as np
    import concourse.bacc as bacc
    from concourse.bass_utils import run_bass_kernel_spmd

    nc = bacc.Bacc("TRN2", target_bir_lowering=False, num_devices=1)
    arrays, args = {}, []
    for name in _INS:
        a = np.ascontiguousarray(inputs[name])
        arrays[f"in_{name}"] = a
        args.append(nc.dram_tensor(f"in_{name}", a.shape, mybir.dt.from_np(a.dtype), kind="ExternalInput").ap())
    args.append(nc.dram_tensor("out_0", (B, T, D), F32, kind="ExternalOutput").ap())
    build(nc, *args)
    r = run_bass_kernel_spmd(nc, [arrays], core_ids=[0])
    return r.results[0]["out_0"]
```
